# Optimizing a Trainium2 kernel written in Bass

```python
import numpy as np
import jax
import jax.numpy as jnp

def _softmax(x, axis=-1):
    return jax.nn.softmax(x, axis=axis)

def _gelu(x):
    return jax.nn.gelu(x, approximate=True)

def _silu(x):
    return jax.nn.silu(x)

def _sigmoid(x):
    return jax.nn.sigmoid(x)

def _layernorm(x, axis=-1, eps=1e-05):
    m = jnp.mean(x, axis=axis, keepdims=True)
    v = jnp.var(x, axis=axis, keepdims=True)
    return (x - m) / jnp.sqrt(v + eps)

def _scatter_add(tgt, idx, src, axis=0):
    return tgt.at[idx].add(src)

def _segment_sum(src, seg, n):
    return jax.ops.segment_sum(src, seg, n)
kernel_name = 'mk_perceiver_d1_seqx_r2_06c047'

def setup_inputs(seed: int=0):
    np.random.seed(seed)
    _w = jnp.asarray

    def _rec_inputs():
        import jax
        import jax.numpy as jnp
        _rk = jax.random.key(seed)
        x = 7.22e-05 + 1 * jax.random.normal(jax.random.fold_in(_rk, 1), (2, 128, 512), jnp.float32)
        _lenS = 128 - jax.random.randint(jax.random.fold_in(_rk, 7), (2,), 0, max(1, 128 // 4) + 1, jnp.int32)
        _lenS2 = 2048 - jax.random.randint(jax.random.fold_in(_rk, 8), (2,), 0, max(1, 2048 // 4) + 1, jnp.int32)
        _ctx_1024P = jax.random.normal(jax.random.fold_in(_rk, 11), (2, 16, 512), jnp.float32)
        _ctx_1024c = jax.random.dirichlet(jax.random.fold_in(_rk, 511), 0.3 * jnp.ones((16,), jnp.float32), (2, 2048))
        _ctx_1024t = jnp.einsum('bsk,bkd->bsd', _ctx_1024c, _ctx_1024P)
        _ctx_1024t = _ctx_1024t * jax.lax.rsqrt(jnp.mean(jnp.square(_ctx_1024t)) + 1e-12) * 0.953939
        ctx_1024 = 4.13588e-05 + 0.999923 * (_ctx_1024t + 0.3 * jax.random.normal(jax.random.fold_in(_rk, 611), (2, 2048, 512), jnp.float32))
        return (x, ctx_1024)
    x, ctx_1024 = _rec_inputs()

    def _L0_xattn_setup():
        import jax, jax.numpy as jnp
        import numpy as np
        DIM = 512
        NHEADS = 16
        HEAD_DIM = DIM // NHEADS

        def _split_heads(x):
            B, S, _ = x.shape
            return x.reshape(B, S, NHEADS, HEAD_DIM).transpose(0, 2, 1, 3)
        key = jax.random.key(seed)
        ks = jax.random.split(key, 11)
        B, S = (4, 1024)
        scale = 1.0 / np.sqrt(DIM)
        inp = {'Q': jax.random.normal(ks[0], (B, S, DIM), jnp.float32), 'K': jax.random.normal(ks[1], (B, S, DIM), jnp.float32), 'V': jax.random.normal(ks[2], (B, S, DIM), jnp.float32), 'Wq': jax.random.normal(ks[3], (DIM, DIM), jnp.float32) * scale, 'bq': jnp.zeros((DIM,), jnp.float32), 'Wk': jax.random.normal(ks[4], (DIM, DIM), jnp.float32) * scale, 'bk': jnp.zeros((DIM,), jnp.float32), 'Wv': jax.random.normal(ks[5], (DIM, DIM), jnp.float32) * scale, 'bv': jnp.zeros((DIM,), jnp.float32), 'Wo': jax.random.normal(ks[6], (DIM, DIM), jnp.float32) * scale, 'bo': jnp.zeros((DIM,), jnp.float32)}
        return inp
    _L0_xattn_all = _L0_xattn_setup()
    _L0_xattn_in = {k: v for k, v in _L0_xattn_all.items() if k in ('Wq', 'bq', 'Wk', 'bk', 'Wv', 'bv', 'Wo', 'bo')}
    del _L0_xattn_all

    def _L0_attn_setup():
        import jax, jax.numpy as jnp
        import numpy as np
        LN_EPS = 1e-05
        NUM_HEAD = 16
        key = jax.random.key(seed)
        ks = jax.random.split(key, 10)
        B, S, E = (2, 1024, 512)
        sc = 0.02
        return {'x': jax.random.normal(ks[0], (B, S, E), jnp.float32), 'wq': jax.random.normal(ks[1], (E, E), jnp.float32) * sc, 'bq': jax.random.normal(ks[2], (E,), jnp.float32) * sc, 'wk': jax.random.normal(ks[3], (E, E), jnp.float32) * sc, 'bk': jax.random.normal(ks[4], (E,), jnp.float32) * sc, 'wv': jax.random.normal(ks[5], (E, E), jnp.float32) * sc, 'bv': jax.random.normal(ks[6], (E,), jnp.float32) * sc, 'wo': jax.random.normal(ks[7], (E, E), jnp.float32) * sc, 'bo': jax.random.normal(ks[8], (E,), jnp.float32) * sc, 'gamma': jnp.ones((E,), jnp.float32), 'beta': jnp.zeros((E,), jnp.float32)}
    _L0_attn_all = _L0_attn_setup()
    _L0_attn_in = {k: v for k, v in _L0_attn_all.items() if k in ('wq', 'bq', 'wk', 'bk', 'wv', 'bv', 'wo', 'bo', 'gamma', 'beta')}
    del _L0_attn_all

    def _L0_ffn_setup():
        import jax, jax.numpy as jnp
        import numpy as np
        H = 512
        I = 2048
        E = 4
        LN_EPS = 1e-12

        def _layer_norm(x, gamma, beta, eps=LN_EPS):
            mu = jnp.mean(x, axis=-1, keepdims=True)
            var = jnp.mean(jnp.square(x - mu), axis=-1, keepdims=True)
            return (x - mu) * jax.lax.rsqrt(var + eps) * gamma + beta
        key = jax.random.key(seed)
        ks = jax.random.split(key, 8)
        B, S = (4, 256)
        scale = 0.02
        return {'hidden_states': jax.random.normal(ks[0], (B, S, H), jnp.float32), 'W_router': jax.random.normal(ks[1], (H, E), jnp.float32) * scale, 'W1': jax.random.normal(ks[2], (E, H, I), jnp.float32) * scale, 'b1': jax.random.normal(ks[3], (E, I), jnp.float32) * scale, 'Wo': jax.random.normal(ks[4], (I, H), jnp.float32) * scale, 'bo': jax.random.normal(ks[5], (H,), jnp.float32) * scale, 'ln_gamma': jnp.ones((H,), jnp.float32), 'ln_beta': jnp.zeros((H,), jnp.float32)}
    _L0_ffn_all = _L0_ffn_setup()
    _L0_ffn_in = {k: v for k, v in _L0_ffn_all.items() if k in ('W_router', 'W1', 'b1', 'Wo', 'bo', 'ln_gamma', 'ln_beta')}
    del _L0_ffn_all
    return {'x': x, 'ctx_1024': ctx_1024, 'L0_xattn_Wq': _L0_xattn_in['Wq'], 'L0_xattn_bq': _L0_xattn_in['bq'], 'L0_xattn_Wk': _L0_xattn_in['Wk'], 'L0_xattn_bk': _L0_xattn_in['bk'], 'L0_xattn_Wv': _L0_xattn_in['Wv'], 'L0_xattn_bv': _L0_xattn_in['bv'], 'L0_xattn_Wo': _L0_xattn_in['Wo'], 'L0_xattn_bo': _L0_xattn_in['bo'], 'L0_attn_wq': _L0_attn_in['wq'], 'L0_attn_bq': _L0_attn_in['bq'], 'L0_attn_wk': _L0_attn_in['wk'], 'L0_attn_bk': _L0_attn_in['bk'], 'L0_attn_wv': _L0_attn_in['wv'], 'L0_attn_bv': _L0_attn_in['bv'], 'L0_attn_wo': _L0_attn_in['wo'], 'L0_attn_bo': _L0_attn_in['bo'], 'L0_attn_gamma': _L0_attn_in['gamma'], 'L0_attn_beta': _L0_attn_in['beta'], 'L0_ffn_W_router': _L0_ffn_in['W_router'], 'L0_ffn_W1': _L0_ffn_in['W1'], 'L0_ffn_b1': _L0_ffn_in['b1'], 'L0_ffn_Wo': _L0_ffn_in['Wo'], 'L0_ffn_bo': _L0_ffn_in['bo'], 'L0_ffn_ln_gamma': _L0_ffn_in['ln_gamma'], 'L0_ffn_ln_beta': _L0_ffn_in['ln_beta']}

def reference(x, ctx_1024, L0_xattn_Wq, L0_xattn_bq, L0_xattn_Wk, L0_xattn_bk, L0_xattn_Wv, L0_xattn_bv, L0_xattn_Wo, L0_xattn_bo, L0_attn_wq, L0_attn_bq, L0_attn_wk, L0_attn_bk, L0_attn_wv, L0_attn_bv, L0_attn_wo, L0_attn_bo, L0_attn_gamma, L0_attn_beta, L0_ffn_W_router, L0_ffn_W1, L0_ffn_b1, L0_ffn_Wo, L0_ffn_bo, L0_ffn_ln_gamma, L0_ffn_ln_beta):
    import jax
    import jax.numpy as jnp

    def _L0_xattn_ref(Q, K, V, Wq, bq, Wk, bk, Wv, bv, Wo, bo):
        import jax, jax.numpy as jnp
        import numpy as np
        DIM = 512
        NHEADS = 16
        HEAD_DIM = DIM // NHEADS

        def _split_heads(x):
            B, S, _ = x.shape
            return x.reshape(B, S, NHEADS, HEAD_DIM).transpose(0, 2, 1, 3)
        q = _split_heads(Q @ Wq + bq)
        k = _split_heads(K @ Wk + bk)
        v = _split_heads(V @ Wv + bv)
        scores = jnp.einsum('bhqd,bhkd->bhqk', q, k) / np.sqrt(HEAD_DIM)
        attn = jax.nn.softmax(scores, axis=-1)
        out = jnp.einsum('bhqk,bhkd->bhqd', attn, v)
        B, H, S, hd = out.shape
        out = out.transpose(0, 2, 1, 3).reshape(B, S, H * hd)
        return out @ Wo + bo

    def _L0_attn_ref(x, wq, bq, wk, bk, wv, bv, wo, bo, gamma, beta):
        import jax, jax.numpy as jnp
        import numpy as np
        LN_EPS = 1e-05
        NUM_HEAD = 16
        B, S, E = x.shape
        H = NUM_HEAD
        D = E // H
        Q = x @ wq + bq
        K = x @ wk + bk
        V = x @ wv + bv
        Q = Q.reshape(B * H, S, D)
        K = K.reshape(B * H, S, D)
        V = V.reshape(B * H, S, D)
        scores = jnp.einsum('bqd,bkd->bqk', Q, K) / jnp.sqrt(jnp.float32(D))
        attn = jax.nn.softmax(scores, axis=-1)
        ctx = jnp.einsum('bqk,bkd->bqd', attn, V)
        ctx = ctx.reshape(B, S, E)
        out = ctx @ wo + bo
        out = out + x
        mu = jnp.mean(out, axis=-1, keepdims=True)
        var = jnp.var(out, axis=-1, keepdims=True)
        out = (out - mu) * jax.lax.rsqrt(var + LN_EPS) * gamma + beta
        return out

    def _L0_ffn_ref(hidden_states, W_router, W1, b1, Wo, bo, ln_gamma, ln_beta):
        import jax, jax.numpy as jnp
        import numpy as np
        H = 512
        I = 2048
        E = 4
        LN_EPS = 1e-12

        def _layer_norm(x, gamma, beta, eps=LN_EPS):
            mu = jnp.mean(x, axis=-1, keepdims=True)
            var = jnp.mean(jnp.square(x - mu), axis=-1, keepdims=True)
            return (x - mu) * jax.lax.rsqrt(var + eps) * gamma + beta
        B, S, _ = hidden_states.shape
        x = hidden_states.reshape(-1, H)
        logits = x @ W_router
        expert_idx = jnp.argmax(logits, axis=-1)
        h = jnp.einsum('th,ehi->tei', x, W1) + b1
        h = jax.nn.gelu(h, approximate=False)
        onehot = jax.nn.one_hot(expert_idx, E, dtype=x.dtype)
        intermediate = jnp.einsum('te,tei->ti', onehot, h)
        y = intermediate @ Wo + bo + x
        y = _layer_norm(y, ln_gamma, ln_beta)
        return y.reshape(B, S, H)
    x = x + _L0_xattn_ref(_layernorm(x, axis=-1), ctx_1024, ctx_1024, L0_xattn_Wq, L0_xattn_bq, L0_xattn_Wk, L0_xattn_bk, L0_xattn_Wv, L0_xattn_bv, L0_xattn_Wo, L0_xattn_bo)
    x = x + _L0_attn_ref(_layernorm(x, axis=-1), L0_attn_wq, L0_attn_bq, L0_attn_wk, L0_attn_bk, L0_attn_wv, L0_attn_bv, L0_attn_wo, L0_attn_bo, L0_attn_gamma, L0_attn_beta)
    x = x + _L0_ffn_ref(_layernorm(x, axis=-1), L0_ffn_W_router, L0_ffn_W1, L0_ffn_b1, L0_ffn_Wo, L0_ffn_bo, L0_ffn_ln_gamma, L0_ffn_ln_beta)
    return x

_drawn_inputs = setup_inputs


def setup_inputs(seed=0):
    import zlib

    import numpy as np

    out = dict(_drawn_inputs(seed))
    spreads = {'L0_xattn_bq': (0.0, 0.375),
     'L0_xattn_bk': (0.0, 0.8),
     'L0_xattn_bv': (0.0, 0.1),
     'L0_xattn_bo': (0.0, 0.1),
     'L0_attn_gamma': (1.0, 0.2),
     'L0_attn_beta': (0.0, 0.1),
     'L0_ffn_ln_gamma': (1.0, 0.2),
     'L0_ffn_ln_beta': (0.0, 0.1)}
    factors = {'L0_attn_wq': 8.0,
     'L0_attn_bq': 8.0,
     'L0_attn_wk': 8.0,
     'L0_attn_bk': 8.0,
     'L0_attn_wv': 3.668,
     'L0_attn_bv': 8.0,
     'L0_attn_wo': 3.634,
     'L0_attn_bo': 5.115,
     'L0_ffn_b1': 8.0,
     'L0_ffn_bo': 8.0}
    for name, (base, spread) in spreads.items():
        noise = np.random.default_rng([zlib.crc32(name.encode()), seed]).standard_normal(out[name].shape)
        drawn = base * np.exp(spread * noise) if base else spread * noise
        out[name] = jnp.asarray(drawn.astype(out[name].dtype))
    for name, factor in factors.items():
        out[name] = (out[name] * factor).astype(out[name].dtype)
    return out
```

```python
from contextlib import ExitStack

import concourse.bass as bass
from concourse import mybir

F32 = mybir.dt.float32
F32R = mybir.dt.float32r
ALU = mybir.AluOpType
ACT = mybir.ActivationFunctionType
AX = mybir.AxisListType

P = 128
KB = 1024
EPS = 1e-5
EPS_FFN = 1e-12


def perceiver_block(nc, a, out):
    B, T, D = a["x"].shape
    S = a["ctxT"].shape[0] // B * a["ctxT"].shape[3]
    H = 16
    DH = D // H
    KT = D // P
    HPG = P // DH
    G = H // HPG
    CH = a["ctxT"].shape[3]
    C = S // CH
    JT = CH // P
    NKT = S // P
    TOK = B * T
    E = a["W_router"].shape[2]
    I = a["W1"].shape[2]
    IT = I // P
    IC = I // CH
    NW1 = E * KT
    SCALE = float(DH) ** -0.5
    NH2 = B * H
    TPH = T // H
    G2 = NH2 // HPG
    assert G == JT and T == P and TPH * H == P and KT == G and IC * B == 8

    with ExitStack() as ctx:
        base = -(-nc.sbuf_base // 32) * 32
        ctx.enter_context(nc.sbuf_tensor("arena", [P, (207 * KB) // 4], F32))

        def at(name, shape, dtype, kb):
            return nc.alloc_sbuf_tensor_at(name, shape, dtype, offset=base + int(kb * KB))

        def sem(name):
            return ctx.enter_context(nc.semaphore(name))

        wkH = at("wkH", [P, KT, D], F32R, 0)
        wkL = at("wkL", [P, KT, D], F32R, 8)
        wvH = at("wvH", [P, KT, D], F32R, 16)
        wvL = at("wvL", [P, KT, D], F32R, 24)
        raw = at("raw", [P, KT, CH], F32, 32)
        ctxH = [at(f"ctxH{i}", [P, KT, CH], F32R, 40 + 8 * i) for i in range(2)]
        ctxL = [at(f"ctxL{i}", [P, KT, CH], F32R, 56 + 8 * i) for i in range(2)]
        PT = at("PT", [P, HPG, NKT, T], F32, 40)
        kH = at("kH", [P, G, S], F32R, 72)
        kL = at("kL", [P, G, S], F32R, 104)
        V = at("V", [P, NKT, D], F32, 136)
        Pm = at("Pm", [P, S], F32, 168)
        qmH = at("qmH", [P, G, HPG, T], F32R, 176)
        qmL = at("qmL", [P, G, HPG, T], F32R, 184)
        x = at("x_sb", [P, B, D], F32, 192)
        qT = at("qT", [P, G, TOK], F32, 196)
        attnT = at("attnT", [P, G, TOK], F32, 200)
        ident = at("ident", [P, P], F32, 204)
        RT = at("RT", [P, T], F32, 204.5)
        rexp = at("rexp", [P, HPG, DH], F32, 205)
        small = at("small", [P, 256], F32, 205.5)
        wq = at("wq", [P, KT, D], F32, 136)
        wk_raw = at("wk_raw", [P, KT, D], F32, 144)
        wv_raw = at("wv_raw", [P, KT, D], F32, 152)
        xn = at("xn", [P, B, D], F32, 160)
        xnT = at("xnT", [P, KT, TOK], F32, 164)
        wo = at("wo", [P, KT, D], F32, 0)
        wq2 = at("wq2", [P, KT, D], F32, 8)
        wk2 = at("wk2", [P, KT, D], F32, 16)
        wv2 = at("wv2", [P, KT, D], F32, 24)
        wo2 = at("wo2", [P, KT, D], F32, 32)
        woF = at("woF", [P, IT, D], F32, 0)
        y = at("y", [P, B, D], F32, 56)
        yT = at("yT", [P, KT, TOK], F32, 44)
        qn = at("qn", [P, B, D], F32, 48)
        kn = at("kn", [P, B, D], F32, 52)
        vn = at("vn", [P, B, D], F32, 40)
        P2 = at("P2", [P, NH2, P], F32, 40)
        cn = at("cn", [P, B, D], F32, 60)
        cT = at("cT", [P, KT, TOK], F32, 64)
        u = at("u", [P, B, D], F32, 68)
        KM = at("KM", [P, G2, HPG, P], F32, 136)
        PT2 = at("PT2", [P, NH2, P], F32, 152)
        Q2 = at("Q2", [P, NH2, DH], F32, 168)
        K2 = at("K2", [P, NH2, DH], F32, 172)
        V2 = at("V2", [P, NH2, DH + 1], F32, 176)
        V2c = at("V2c", [P, NH2, DH], F32, 181)
        QT2 = at("QT2", [P, G2, P], F32, 185)
        c2 = at("c2", [P, NH2, DH], F32, 172)
        w1raw = [at(f"w1raw{i}", [P, I], F32, 72 + 8 * i) for i in range(2)]
        w1H = [at(f"w1H{i}", [P, I], F32R, 88 + 8 * i) for i in range(2)]
        w1L = [at(f"w1L{i}", [P, I], F32R, 104 + 8 * i) for i in range(2)]
        rows = at("rows", [P, 8, D], F32, 120)
        rows2 = at("rows2", [P, 2, D], F32, 196)
        zm = at("zm", [P, B, D], F32, 60)
        zH = at("zH", [P, NW1, TOK], F32R, 136)
        zL = at("zL", [P, NW1, TOK], F32R, 152)
        hid = at("hid", [P, B, I], F32, 168)
        hidT = at("hidT", [P, IT, TOK], F32, 40)
        wr = at("wr", [P, KT, E], F32, 191)
        b1raw = at("b1raw", [E, I], F32, 32)
        b1H = at("b1H", [E, I], F32R, 168)
        b1L = at("b1L", [E, I], F32R, 176)
        ohT = at("ohT", [E, B, P], F32R, 189.5)
        x2 = at("x2", [P, B, D], F32, 200)

        col = [0]

        def cols(n):
            col[0] += n
            assert col[0] <= 256
            return small[:, col[0] - n:col[0]]

        stats = cols(B * 6).rearrange("p (b s) -> p b s", b=B)
        meanvar = cols(B * 2).rearrange("p (b s) -> p b s", b=B)
        vareps = cols(B)
        rstd = cols(B)
        minus_half = cols(B)
        bqs = cols(G)
        bias3 = cols(3 * G).rearrange("p (k g) -> p k g", k=3)
        mx = cols(2 * C).rearrange("p (k c) -> p k c", k=2)
        nmax = cols(2)
        den = cols(H * C).rearrange("p (h c) -> p h c", h=H)
        dsum = cols(HPG)
        recip = cols(HPG)
        mx2 = cols(NH2)
        recip2 = cols(NH2)
        logit = cols(B * E).rearrange("p (b e) -> p b e", b=B)
        lmax = cols(B)
        order = cols(E)
        rank = cols(B * E).rearrange("p (b e) -> p b e", b=B)
        rmax = cols(B)
        onehot = cols(B * E).rearrange("p (b e) -> p b e", b=B)

        ps = ctx.enter_context(nc.psum_tensor("ps", [P, 8, CH], F32))
        PT_BANKS = (4, 5, 6)
        PV_BANK = 7
        QKV_BANKS = (4, 5, 6, 7, 0, 1)

        x_in, wq_in, wk_in, wv_in, bias_in = (sem(n) for n in ("x_in", "wq_in", "wk_in", "wv_in", "bias_in"))
        raw_in = sem("raw_in")
        wo_in, wqkv2_in, wo2_in, rows_in, w1_in0, w1_in1, woF_in, wr_in, b1_in = (
            sem(n) for n in ("wo_in", "wqkv2_in", "wo2_in", "rows_in", "w1_in0", "w1_in1", "woF_in", "wr_in", "b1_in"))
        w1_in = [w1_in0, w1_in1]
        ident_done, zero_done, half_done = sem("ident_done"), sem("zero_done"), sem("half_done")
        var_done, rstd_done, norm_done = sem("var_done"), sem("rstd_done"), sem("norm_done")
        xT_mm, xT_done, q_mm = sem("xT_mm"), sem("xT_done"), sem("q_mm")
        wk_split, wv_hi, wv_split, bq_scaled = sem("wk_split"), sem("wv_hi"), sem("wv_split"), sem("bq_scaled")
        ctx_hi, ctx_split = sem("ctx_hi"), sem("ctx_split")
        k_mm, k_hi, k_lo = sem("k_mm"), sem("k_hi"), sem("k_lo")
        v_mm = sem("v_mm")
        v_done = sem("v_done")
        qm_hi, qm_done = sem("qm_hi"), sem("qm_done")
        s_mm, max_part, max_done = sem("s_mm"), sem("max_part"), sem("max_done")
        exp_done, t_mm = sem("exp_done"), sem("t_mm")
        pt_act, pt_dve = sem("pt_act"), sem("pt_dve")
        pv_mm, rexp_done, r_mm, r_copied, o_done = (
            sem(n) for n in ("pv_mm", "rexp_done", "r_mm", "r_copied", "o_done"))
        dve_step = sem("dve_step")
        wo_mm, yT_mm, yT_done, qkv_mm, qkv_ready = (sem(n) for n in ("wo_mm", "yT_mm", "yT_done", "qkv_mm", "qkv_ready"))
        c2_ready, ones_ready, v2_ready, q2T_mm, k2T_mm = (sem(n) for n in ("c2_ready", "ones_ready", "v2_ready", "q2T_mm", "k2T_mm"))
        qt2_ready, km_zero, km_ready, s2_mm, sub2_done = (sem(n) for n in ("qt2_ready", "km_zero", "km_ready", "s2_mm", "sub2_done"))
        exp2_done, p2T_mm, pt2_act, pt2_dve, pv2_mm = (sem(n) for n in ("exp2_done", "p2T_mm", "pt2_act", "pt2_dve", "pv2_mm"))
        cT_mm, cT_done, o2_mm, x2T_mm, x2T_done = (sem(n) for n in ("cT_mm", "cT_done", "o2_mm", "x2T_mm", "x2T_done"))
        logit_mm, z_ready, ohT_mm, ohT_ready, zT_mm = (sem(n) for n in ("logit_mm", "z_ready", "ohT_mm", "ohT_ready", "zT_mm"))
        z_hi, z_split, w1_hi, w1_split, b1_hi = (sem(n) for n in ("z_hi", "z_split", "w1_hi", "w1_split", "b1_hi"))
        b1_split, w1_tile, w1_mm, gelu_done, hT_mm = (sem(n) for n in ("b1_split", "w1_tile", "w1_mm", "gelu_done", "hT_mm"))
        hT_act, hT_dve, f_mm, out_ready, stored = (sem(n) for n in ("hT_act", "hT_dve", "f_mm", "out_ready", "stored"))
        scratch_out = [sem(f"scratch_out{k}") for k in range(4)]
        scratch_in = [sem(f"scratch_in{k}") for k in range(4)]

        scratch = nc.dram_tensor("scratch", [4, TOK, D], F32, kind="Internal").ap()
        by_token = [scratch[k].rearrange("(b t) n -> t b n", b=B) for k in range(4)]
        by_position = [scratch[k].rearrange("(h t) (c d) -> (t c) h d", t=TPH, d=DH) for k in range(4)]

        block = ctx.enter_context(nc.Block())


        @block.sync
        def _(sp):
            sp.dma_start(x[:], a["x"].rearrange("b t d -> t b d")).then_inc(x_in, 16)
            sp.dma_start(bias3, a["bias3"]).then_inc(bias_in, 16)
            sp.dma_start(wk_raw[:], a["xWk"]).then_inc(wk_in, 16)
            sp.dma_start(wq[:], a["xWq"]).then_inc(wq_in, 16)
            sp.dma_start(raw[:], a["ctxT"][0]).then_inc(raw_in, 16)
            sp.dma_start(wv_raw[:], a["xWv"]).then_inc(wv_in, 16)
            with sp.Fori(1, B * C) as k:
                sp.wait_ge(ctx_split, k)
                sp.dma_start(raw[:], a["ctxT"][bass.ds(k, 1)].rearrange("a p k s -> (a p) k s")).then_inc(raw_in, 16)

            sp.wait_ge(v_mm, B * C * JT)
            sp.wait_ge(ctx_split, B * C)
            for t, n, s in ((wo, "xWo", wo_in), (wq2, "wq", wqkv2_in), (wk2, "wk", wqkv2_in),
                            (wv2, "wv", wqkv2_in), (wo2, "wo", wo2_in)):
                sp.dma_start(t[:], a[n]).then_inc(s, 16)
            sp.wait_ge(s_mm, B * H * C)
            for n in range(8):
                sp.dma_start(rows[:, n, :], a["rows"][n:n + 1, :].to_broadcast([P, D])).then_inc(rows_in, 16)
            for n in range(2):
                sp.dma_start(rows2[:, n, :], a["rows"][8 + n:9 + n, :].to_broadcast([P, D])).then_inc(rows_in, 16)
            w1_v = a["W1"].rearrange("e (k p) i -> (e k) p i", p=P)
            for n in range(2):
                sp.dma_start(w1raw[n][:], w1_v[n]).then_inc(w1_in[n], 16)
            for k, src in enumerate((qn, kn, vn)):
                sp.wait_ge(qkv_ready, B * (k + 1))
                sp.dma_start(by_token[k], src[:]).then_inc(scratch_out[k], 16)
            for k, dst in enumerate((Q2, K2, V2c)):
                sp.wait_ge(scratch_out[k], 16)
                sp.dma_start(dst[:], by_position[k]).then_inc(scratch_in[k], 16)
            sp.wait_ge(c2_ready, 1)
            sp.dma_start(by_position[3], c2[:]).then_inc(scratch_out[3], 16)
            sp.wait_ge(scratch_out[3], 16)
            sp.dma_start(cn[:], by_token[3]).then_inc(scratch_in[3], 16)
            sp.wait_ge(o2_mm, B)
            sp.dma_start(wr[:], a["W_router"]).then_inc(wr_in, 16)
            sp.dma_start(b1raw[:], a["b1"]).then_inc(b1_in, 16)
            for n in range(2, NW1):
                sp.wait_ge(w1_split, n - 1)
                sp.dma_start(w1raw[n % 2][:], w1_v[n]).then_inc(w1_in[n % 2], 16)
                if n == 3:
                    sp.dma_start(woF[:], a["ffn_Wo"]).then_inc(woF_in, 16)
            for b in range(B):
                sp.wait_ge(out_ready, b + 1)
                sp.dma_start(out[b], u[:, b, :]).then_inc(stored, 16)
            sp.wait_ge(stored, 16 * B)

        @block.gpsimd
        def _(pool):
            pool.memset(ident[:], 0.0).then_inc(ident_done, 1)
            pool.memset(minus_half, -0.5).then_inc(half_done, 1)
            pool.memset(qmH[:].bitcast(F32), 0.0).then_inc(zero_done, 1)
            pool.memset(qmL[:].bitcast(F32), 0.0).then_inc(zero_done, 1)
            for e in range(E):
                pool.memset(order[:, e:e + 1], float(E - e)).then_inc(half_done, 1)
            pool.wait_ge(ident_done, 1)
            pool.affine_select(out=ident[:], in_=ident[:], compare_op=ALU.not_equal, fill=1.0, base=0,
                               pattern=[[-1, P]], channel_multiplier=1).then_inc(ident_done, 1)

            def rsqrt(n):
                pool.wait_ge(half_done, 1 + E)
                pool.wait_ge(var_done, n + 1)
                pool.tensor_tensor(rstd, vareps, minus_half, ALU.pow).then_inc(rstd_done, 1)

            rsqrt(0)
            pool.wait_ge(wv_hi, 1)
            pool.tensor_tensor(wvL[:], wv_raw[:], wvH[:].bitcast(F32), ALU.subtract).then_inc(wv_split, 1)
            pool.wait_ge(zero_done, 2)
            pool.wait_ge(wv_split, 1)
            pool.wait_ge(v_done, G)
            for b in range(B):
                if b:
                    pool.wait_ge(s_mm, b * (H * C))
                for i in range(HPG):
                    q = slice(DH * i, DH * (i + 1))
                    if b or i:
                        pool.wait_ge(qm_done, b * HPG + i)
                    pool.tensor_copy(qmH[q, :, i, :], qT[q, :, b * T:(b + 1) * T]).then_inc(qm_hi, 1)
                    pool.wait_ge(qm_hi, b * HPG + i + 1)
                    pool.tensor_tensor(qmL[q, :, i, :], qT[q, :, b * T:(b + 1) * T],
                                       qmH[q, :, i, :].bitcast(F32), ALU.subtract).then_inc(qm_done, 1)
            pool.wait_ge(qm_done, B * HPG)
            for n in range(1, 5):
                rsqrt(n)
                if n == 1:
                    pool.wait_ge(pv_mm, B * G)
                    pool.memset(KM[:], 0.0).then_inc(km_zero, 1)
                    pool.wait_ge(km_zero, 1)

        @block.scalar
        def _(act):
            for b in range(B):
                act.wait_ge(xT_mm, b + 1)
                act.copy(xnT[:, :, b * T:(b + 1) * T],
                         ps[:, b, :].rearrange("p (k t) -> p k t", k=KT)).then_inc(xT_done, 1)
            act.wait_ge(wv_in, 16)
            act.copy(wvH[:], wv_raw[:]).then_inc(wv_hi, 1)
            act.wait_ge(bq_scaled, 1)
            for m in range(G):
                act.wait_ge(q_mm, m + 1)
                act.activation(qT[:, m, :], ps[:, 4 + m, 0:TOK], ACT.Identity, bias=bqs[:, m:m + 1],
                               scale=SCALE).then_inc(v_done, 1)
            with act.Fori(0, B) as b:
                with act.Fori(0, C) as c:
                    for m in range(G):
                        act.wait_ge(k_mm, b * (C * G) + c * G + (m + 1))
                        act.activation(kH[:, m, bass.ds(c * CH, CH)], ps[:, m, :], ACT.Identity,
                                       bias=bias3[:, 1, m:m + 1]).then_inc(k_hi, 1)
                    for j in range(JT):
                        act.wait_ge(v_mm, b * (C * JT) + c * JT + (j + 1))
                        act.copy(V[:, bass.ds(c * JT + j, 1), :].rearrange("p a n -> p (a n)"), ps[:, 4 + j, :]).then_inc(v_done, 1)

                def pt_copies(h):
                    g, i = divmod(h, HPG)
                    for c in range(0, C, 2):
                        act.wait_ge(t_mm, b * (H * C) + (C * h + c + 1))
                        if g == 0:
                            act.wait_ge(v_mm, (b + 1) * (C * JT))
                        else:
                            act.wait_ge(pv_mm, b * G + g)
                        act.copy(PT[:, i, c * JT:(c + 1) * JT, :].rearrange("p k t -> p (k t)"),
                                 ps[:, PT_BANKS[(C * h + c) % 3], :]).then_inc(pt_act, 1)

                for h in range(H):
                    act.wait_ge(max_done, b * H + (h + 1))
                    for c in range(C):
                        if h:
                            act.wait_ge(t_mm, b * (H * C) + (C * (h - 1) + c + 1))
                        act.activation(Pm[:, c * CH:(c + 1) * CH], ps[:, c, :], ACT.Exp, bias=nmax[:, h % 2:h % 2 + 1],
                                       accum_out=den[:, h, c:c + 1]).then_inc(exp_done, 1)
                    pt_copies(h)
                    if h and h % HPG == 0:
                        act.wait_ge(r_mm, b * G + h // HPG)
                        act.copy(RT[:], ps[:, PV_BANK, P:2 * P]).then_inc(r_copied, 1)
                act.wait_ge(r_mm, (b + 1) * G)
                act.copy(RT[:], ps[:, PV_BANK, P:2 * P]).then_inc(r_copied, 1)
                act.wait_ge(s_mm, (b + 1) * (H * C))
                act.wait_ge(pv_mm, (b + 1) * G)
                act.wait_ge(t_mm, (b + 1) * (H * C))

            def transposed(dst, sem_in, n_in, bank, sem_out):
                for b in range(B):
                    act.wait_ge(sem_in, n_in + b + 1)
                    act.copy(dst[:, :, b * T:(b + 1) * T],
                             ps[:, bank + b, :].rearrange("p (k t) -> p k t", k=KT)).then_inc(sem_out, 1)

            transposed(yT, yT_mm, 0, 2, yT_done)
            act.wait_ge(q2T_mm, 1)
            act.copy(QT2[:].rearrange("p g t -> p (g t)"), ps[:, 0:2, :].rearrange("p a n -> p (a n)")).then_inc(qt2_ready, 1)
            for n in range(G2 + 3):
                if n < G2:
                    act.wait_ge(sub2_done, n + 1)
                    act.activation(P2[:, HPG * n:HPG * (n + 1), :], P2[:, HPG * n:HPG * (n + 1), :],
                                   ACT.Exp, scale=SCALE).then_inc(exp2_done, 1)
                g = n - 3
                if g >= 0 and g % 2 == 0:
                    act.wait_ge(p2T_mm, g + 1)
                    act.copy(PT2[:, HPG * g:HPG * (g + 1), :].rearrange("p h t -> p (h t)"),
                             ps[:, 4 + g % 4, :]).then_inc(pt2_act, 1)
            transposed(cT, cT_mm, 0, 2, cT_done)
            transposed(yT, x2T_mm, 0, 2, x2T_done)
            for e in range(E):
                for b in range(B):
                    act.wait_ge(zT_mm, B * e + b + 1)
                    act.copy(zH[:, KT * e:KT * (e + 1), b * T:(b + 1) * T],
                             ps[:, b, :].rearrange("p (k t) -> p k t", k=KT)).then_inc(z_hi, 1)
            for b in range(B):
                for c in range(IC):
                    act.wait_ge(w1_mm, IC * b + c + 1)
                    act.activation(hid[:, b, c * CH:(c + 1) * CH], ps[:, IC * b + c, :], ACT.Gelu)\
                       .then_inc(gelu_done, 1)
            for n in range(0, IT // 2, 2):
                act.wait_ge(hT_mm, n + 1)
                act.copy(hidT[:, 2 * n:2 * n + 2, :].rearrange("p k t -> p (k t)"), ps[:, n % 4, :])\
                   .then_inc(hT_act, 1)

        @block.vector
        def _(dve):
            steps = [0]

            def step(ins):
                steps[0] += 1
                ins.then_inc(dve_step, 1)
                dve.wait_ge(dve_step, steps[0])

            def variance(src, eps, b):
                step(dve.bn_stats(stats[:, b, :], src[:, b, :]))
                step(dve.bn_aggr(meanvar[:, b, :], stats[:, b, :]))

            def layernorm(src, dst, eps, n):
                for b in range(B):
                    variance(src, eps, b)
                if n:
                    dve.wait_ge(norm_done, B * n)
                dve.tensor_scalar(vareps, meanvar[:, :, 1], eps, None, ALU.add).then_inc(var_done, 1)
                dve.wait_ge(rstd_done, n + 1)
                for b in range(B):
                    dve.tensor_scalar(dst[:, b, :], src[:, b, :], meanvar[:, b, 0:1], rstd[:, b:b + 1],
                                      ALU.subtract, ALU.mult).then_inc(norm_done, 1)
                dve.wait_ge(norm_done, B * (n + 1))

            dve.wait_ge(x_in, 16)
            layernorm(x, xn, EPS, 0)
            dve.wait_ge(wk_in, 16)
            step(dve.tensor_copy(wkH[:], wk_raw[:]))
            dve.tensor_tensor(wkL[:], wk_raw[:], wkH[:].bitcast(F32), ALU.subtract).then_inc(wk_split, 1)

            dve.wait_ge(bias_in, 16)
            dve.tensor_scalar(bqs, bias3[:, 0, :], SCALE, None, ALU.mult).then_inc(bq_scaled, 1)

            with dve.Fori(0, B) as b:
                def split(c):
                    dve.wait_ge(raw_in, b * (16 * C) + 16 * (c + 1))
                    if c >= 2:
                        dve.wait_ge(v_mm, b * (C * JT) + JT * (c - 1))
                    dve.tensor_copy(ctxH[c % 2][:], raw[:]).then_inc(ctx_hi, 1)
                    dve.wait_ge(ctx_hi, b * C + (c + 1))
                    dve.tensor_tensor(ctxL[c % 2][:], raw[:], ctxH[c % 2][:].bitcast(F32),
                                      ALU.subtract).then_inc(ctx_split, 1)

                split(0)
                for c in range(C):
                    if c + 1 < C:
                        split(c + 1)
                    for m in range(G):
                        dve.wait_ge(k_hi, b * (C * G) + (c * G + m + 1))
                        dve.scalar_tensor_tensor(out=kL[:, m, c * CH:(c + 1) * CH], in0=ps[:, m, :],
                                                 scalar=bias3[:, 1, m:m + 1],
                                                 in1=kH[:, m, c * CH:(c + 1) * CH].bitcast(F32),
                                                 op0=ALU.add, op1=ALU.subtract).then_inc(k_lo, 1)

                def maxima(h):
                    for c in range(C):
                        dve.wait_ge(s_mm, b * (H * C) + (C * h + c + 1))
                        dve.tensor_reduce(mx[:, h % 2, c:c + 1], ps[:, c, :], AX.X, ALU.max).then_inc(max_part, 1)
                    dve.wait_ge(max_part, b * (H * C) + C * (h + 1))
                    dve.tensor_reduce(nmax[:, h % 2:h % 2 + 1], mx[:, h % 2, :], AX.X, ALU.max,
                                      negate=True).then_inc(max_done, 1)

                def pt_copies(h):
                    g, i = divmod(h, HPG)
                    for c in range(1, C, 2):
                        dve.wait_ge(t_mm, b * (H * C) + (C * h + c + 1))
                        if g == 0:
                            dve.wait_ge(v_mm, (b + 1) * (C * JT))
                        else:
                            dve.wait_ge(pv_mm, b * G + g)
                        dve.tensor_copy(PT[:, i, c * JT:(c + 1) * JT, :].rearrange("p k t -> p (k t)"),
                                        ps[:, PT_BANKS[(C * h + c) % 3], :]).then_inc(pt_dve, 1)

                def reciprocals(g):
                    dve.wait_ge(exp_done, b * (H * C) + C * HPG * (g + 1))
                    dve.tensor_reduce(dsum, den[:, HPG * g:HPG * (g + 1), :], AX.X, ALU.add).then_inc(rexp_done, 1)
                    dve.wait_ge(rexp_done, b * (3 * G) + (3 * g + 1))
                    dve.reciprocal(recip, dsum).then_inc(rexp_done, 1)
                    dve.wait_ge(rexp_done, b * (3 * G) + (3 * g + 2))
                    if g:
                        dve.wait_ge(r_mm, b * G + g)
                    dve.tensor_copy(rexp[:], recip.rearrange("p (h o) -> p h o", o=1).to_broadcast([P, HPG, DH]))\
                       .then_inc(rexp_done, 1)

                def outputs(g):
                    dve.wait_ge(r_copied, b * G + (g + 1))
                    dve.wait_ge(pv_mm, b * G + (g + 1))
                    dst = attnT[:, g, bass.ds(b * T, T)]
                    dve.tensor_tensor(dst, ps[:, PV_BANK, 0:T], RT[:], ALU.mult).then_inc(o_done, 1)
                    dve.wait_ge(o_done, b * (2 * G) + (2 * g + 1))
                    dve.tensor_scalar(dst, dst, bias3[:, 2, g:g + 1], None, ALU.add).then_inc(o_done, 1)

                for h in range(H):
                    maxima(h)
                    if h and h % HPG == 0:
                        reciprocals(h // HPG - 1)
                    if h:
                        pt_copies(h - 1)
                    if h > 1 and h % HPG == 1:
                        outputs(h // HPG - 1)
                reciprocals(G - 1)
                pt_copies(H - 1)
                outputs(G - 1)
                dve.wait_ge(pv_mm, (b + 1) * G)
                dve.wait_ge(r_mm, (b + 1) * G)

            R = {n: rows[:, k, :] for k, n in enumerate(("xbo", "bq", "bk", "bv", "bo", "gamma", "beta", "fbo"))}
            dve.wait_ge(rows_in, 160)
            for b in range(B):
                dve.wait_ge(wo_mm, b + 1)
                step(dve.tensor_tensor(u[:, b, :], ps[:, b, :], R["xbo"], ALU.add))
                step(dve.tensor_tensor(x[:, b, :], x[:, b, :], u[:, b, :], ALU.add))
            layernorm(x, y, EPS, 1)
            for k, (dst, bias) in enumerate(((qn, "bq"), (kn, "bk"), (vn, "bv"))):
                for b in range(B):
                    dve.wait_ge(qkv_mm, B * k + b + 1)
                    dve.tensor_tensor(dst[:, b, :], ps[:, QKV_BANKS[B * k + b], :], R[bias], ALU.add).then_inc(qkv_ready, 1)
            dve.wait_ge(scratch_in[2], 16)
            dve.memset(V2[:, :, DH:DH + 1], 1.0).then_inc(v2_ready, 1)
            dve.tensor_copy(V2[:, :, 0:DH], V2c[:]).then_inc(v2_ready, 1)
            dve.wait_ge(km_zero, 1)
            dve.wait_ge(k2T_mm, 1)
            kps = ps[:, 2:4, :].rearrange("p a (g t) -> p (a g) t", t=P)
            for i in range(HPG):
                q = slice(DH * i, DH * (i + 1))
                dve.tensor_copy(KM[q, :, i, :], kps[q, :, :]).then_inc(km_ready, 1)
            dve.wait_ge(scratch_in[0], 16)
            for n in range(G2 + 3):
                if n < G2:
                    bank = ps[:, 4 + n % 4, :].rearrange("p (h t) -> p h t", h=HPG)
                    m = mx2[:, HPG * n:HPG * (n + 1)]
                    dve.wait_ge(s2_mm, n + 1)
                    step(dve.tensor_reduce(m, bank, AX.X, ALU.max))
                    dve.tensor_tensor(P2[:, HPG * n:HPG * (n + 1), :], bank,
                                      m.rearrange("p (h o) -> p h o", o=1).to_broadcast([P, HPG, P]),
                                      ALU.subtract).then_inc(sub2_done, 1)
                g = n - 3
                if g >= 0 and g % 2:
                    dve.wait_ge(p2T_mm, g + 1)
                    dve.tensor_copy(PT2[:, HPG * g:HPG * (g + 1), :].rearrange("p h t -> p (h t)"),
                                    ps[:, 4 + g % 4, :]).then_inc(pt2_dve, 1)
            dve.wait_ge(pv2_mm, 1)
            o2 = ps[:, 0:4, 0:8 * (DH + 1)].rearrange("p a (h d) -> p a h d", h=8)
            step(dve.reciprocal(recip2.rearrange("p (a h o) -> p a h o", a=4, o=1), o2[:, :, :, DH:DH + 1]))
            dve.tensor_tensor(c2[:].rearrange("p (a h) d -> p a h d", a=4), o2[:, :, :, 0:DH],
                              recip2.rearrange("p (a h o) -> p a h o", a=4, o=1).to_broadcast([P, 4, 8, DH]),
                              ALU.mult).then_inc(c2_ready, 1)
            for b in range(B):
                dve.wait_ge(o2_mm, b + 1)
                step(dve.tensor_tensor(u[:, b, :], ps[:, 4 + b, :], R["bo"], ALU.add))
                step(dve.tensor_tensor(u[:, b, :], u[:, b, :], y[:, b, :], ALU.add))
            layernorm(u, u, EPS, 2)
            for b in range(B):
                step(dve.tensor_tensor(u[:, b, :], u[:, b, :], R["gamma"], ALU.mult))
                step(dve.tensor_tensor(u[:, b, :], u[:, b, :], R["beta"], ALU.add))
                step(dve.tensor_tensor(x2[:, b, :], x[:, b, :], u[:, b, :], ALU.add))
            layernorm(x2, y, EPS, 3)
            dve.wait_ge(half_done, 1 + E)
            for b in range(B):
                dve.wait_ge(logit_mm, b + 1)
                step(dve.tensor_copy(logit[:, b, :], ps[:, 4 + b, 0:E]))
                step(dve.tensor_reduce(lmax[:, b:b + 1], logit[:, b, :], AX.X, ALU.max))
                step(dve.tensor_scalar(rank[:, b, :], logit[:, b, :], lmax[:, b:b + 1], None, ALU.is_ge))
                step(dve.tensor_tensor(rank[:, b, :], rank[:, b, :], order, ALU.mult))
                step(dve.tensor_reduce(rmax[:, b:b + 1], rank[:, b, :], AX.X, ALU.max))
                step(dve.tensor_scalar(onehot[:, b, :], rank[:, b, :], rmax[:, b:b + 1], None, ALU.is_equal))
            for e in range(E):
                for b in range(B):
                    if e:
                        dve.wait_ge(zT_mm, B * (e - 1) + b + 1)
                    dve.tensor_scalar(zm[:, b, :], y[:, b, :], onehot[:, b, e:e + 1], None, ALU.mult)\
                       .then_inc(z_ready, 1)
                if e == 0:
                    dve.wait_ge(ohT_mm, 1)
                    dve.tensor_copy(ohT[:], ps[0:E, 6, 0:TOK].rearrange("p (b t) -> p b t", b=B))\
                       .then_inc(ohT_ready, 1)
                for b in range(B):
                    dve.wait_ge(z_hi, B * e + b + 1)
                    dve.tensor_tensor(zL[:, KT * e:KT * (e + 1), b * T:(b + 1) * T],
                                      ps[:, b, :].rearrange("p (k t) -> p k t", k=KT),
                                      zH[:, KT * e:KT * (e + 1), b * T:(b + 1) * T].bitcast(F32),
                                      ALU.subtract).then_inc(z_split, 1)
            dve.wait_ge(b1_in, 16)
            dve.tensor_copy(b1H[:], b1raw[:]).then_inc(b1_split, 1)
            dve.wait_ge(b1_split, 1)
            dve.tensor_tensor(b1L[:], b1raw[:], b1H[:].bitcast(F32), ALU.subtract).then_inc(b1_split, 1)
            for n in range(NW1):
                dve.wait_ge(w1_in[n % 2], 16 * (n // 2 + 1))
                if n >= 2:
                    dve.wait_ge(w1_tile, n - 1)
                dve.tensor_copy(w1H[n % 2][:], w1raw[n % 2][:]).then_inc(w1_hi, 1)
                dve.wait_ge(w1_hi, n + 1)
                dve.tensor_tensor(w1L[n % 2][:], w1raw[n % 2][:], w1H[n % 2][:].bitcast(F32),
                                  ALU.subtract).then_inc(w1_split, 1)
            for n in range(1, IT // 2, 2):
                dve.wait_ge(hT_mm, n + 1)
                dve.tensor_copy(hidT[:, 2 * n:2 * n + 2, :].rearrange("p k t -> p (k t)"), ps[:, n % 4, :])\
                   .then_inc(hT_dve, 1)
            for b in range(B):
                dve.wait_ge(f_mm, b + 1)
                step(dve.tensor_tensor(u[:, b, :], ps[:, 4 + b, :], R["fbo"], ALU.add))
                step(dve.tensor_tensor(u[:, b, :], u[:, b, :], y[:, b, :], ALU.add))
            layernorm(u, u, EPS_FFN, 4)
            for b in range(B):
                step(dve.tensor_tensor(u[:, b, :], u[:, b, :], rows2[:, 0, :], ALU.mult))
                step(dve.tensor_tensor(u[:, b, :], u[:, b, :], rows2[:, 1, :], ALU.add))
                dve.tensor_tensor(u[:, b, :], x2[:, b, :], u[:, b, :], ALU.add).then_inc(out_ready, 1)

        @block.tensor
        def _(pe):
            def transposes(src, banks, sem_out, ready=None):
                for b in range(B):
                    if ready:
                        pe.wait_ge(ready[0], ready[1] + b + 1)
                    for k in range(KT):
                        last = pe.transpose(ps[:, banks[b], k * T:(k + 1) * T], src[:, b, k * P:(k + 1) * P], ident[:])
                    last.then_inc(sem_out, 1)

            def product(dst, pairs):
                for n, (l, r) in enumerate(pairs):
                    mm = pe.matmul(dst, l, r, start=(n == 0), stop=(n == len(pairs) - 1))
                return mm

            pe.wait_ge(ident_done, 2)
            transposes(xn, (0, 1), xT_mm, (norm_done, 0))
            pe.wait_ge(xT_done, B)
            pe.wait_ge(wq_in, 16)
            for m in range(G):
                product(ps[:, 4 + m, 0:TOK], [(wq[:, k, m * P:(m + 1) * P], xnT[:, k, :]) for k in range(KT)])\
                    .then_inc(q_mm, 1)
            pe.wait_ge(wk_split, 1)
            pe.wait_ge(v_done, G)
            with pe.Fori(0, B) as b:
                with pe.Fori(0, C // 2) as cc:
                    for half in range(2):
                        cH, cL = ctxH[half], ctxL[half]
                        pe.wait_ge(ctx_split, b * C + cc * 2 + (half + 1))
                        for m in range(G):
                            f = slice(m * P, (m + 1) * P)
                            product(ps[:, m, :], [(w[:, k, f], c[:, k, :]) for k in range(KT)
                                                  for w, c in ((wkH, cH), (wkL, cH), (wkH, cL))]).then_inc(k_mm, 1)
                        pe.wait_ge(wv_split, 1)
                        pe.wait_ge(v_done, b * (C * JT) + cc * (2 * JT) + (half + 1) * JT)
                        for j in range(JT):
                            t = slice(j * P, (j + 1) * P)
                            product(ps[:, 4 + j, :], [(c[:, k, t], w[:, k, :]) for k in range(KT)
                                                      for c, w in ((cH, wvH), (cH, wvL), (cL, wvH))]).then_inc(v_mm, 1)
                        pe.wait_ge(k_lo, b * (C * G) + cc * (2 * G) + (half + 1) * G)

                pe.wait_ge(qm_done, (b + 1) * HPG)
                pe.wait_ge(v_done, (b + 1) * (C * JT) + JT)

                def scores(h):
                    g, i = divmod(h, HPG)
                    for c in range(C):
                        if h:
                            pe.wait_ge(exp_done, b * (H * C) + (C * (h - 1) + c + 1))
                        kk = slice(c * CH, (c + 1) * CH)
                        product(ps[:, c, :], [(qmH[:, g, i, :], kH[:, g, kk]), (qmH[:, g, i, :], kL[:, g, kk]),
                                              (qmL[:, g, i, :], kH[:, g, kk])]).then_inc(s_mm, 1)

                def transpose_probs(h):
                    for c in range(C):
                        t = C * h + c
                        pe.wait_ge(exp_done, b * (H * C) + (t + 1))
                        if t >= 3:
                            pe.wait_ge(pt_dve if (t - 3) % 2 else pt_act, b * (H * C // 2) + ((t - 3) // 2 + 1))
                        for j in range(JT):
                            last = pe.transpose(ps[:, PT_BANKS[t % 3], j * P:(j + 1) * P],
                                                Pm[:, c * CH + j * P:c * CH + (j + 1) * P], ident[:])
                        last.then_inc(t_mm, 1)

                def weighted_values(g):
                    pe.wait_ge(pt_act, b * (H * C // 2) + HPG * C // 2 * (g + 1))
                    pe.wait_ge(pt_dve, b * (H * C // 2) + HPG * C // 2 * (g + 1))
                    if g:
                        pe.wait_ge(o_done, b * (2 * G) + 2 * g)
                    for n in range(NKT):
                        for i in range(HPG):
                            q = slice(DH * i, DH * (i + 1))
                            last = pe.matmul(ps[q, PV_BANK, 0:T], V[:, n, (HPG * g + i) * DH:(HPG * g + i + 1) * DH],
                                             PT[:, i, n, :], start=(n == 0), stop=(n == NKT - 1))
                    last.then_inc(pv_mm, 1)
                    pe.wait_ge(rexp_done, b * (3 * G) + 3 * (g + 1))
                    pe.matmul(ps[:, PV_BANK, P:2 * P], rexp[:].rearrange("p h d -> p (h d)"), ident[:],
                              start=True, stop=True).then_inc(r_mm, 1)

                for h in range(H):
                    scores(h)
                    if h > 1 and h % HPG == 1:
                        weighted_values(h // HPG - 1)
                    if h:
                        transpose_probs(h - 1)
                transpose_probs(H - 1)
                weighted_values(G - 1)
                pe.wait_ge(exp_done, (b + 1) * (H * C))
                pe.wait_ge(o_done, (b + 1) * (2 * G))

            pe.wait_ge(wo_in, 16)
            pe.wait_ge(o_done, B * 2 * G)
            pe.wait_ge(exp_done, B * H * C)
            for b in range(B):
                product(ps[:, b, :], [(attnT[:, k, b * T:(b + 1) * T], wo[:, k, :]) for k in range(KT)])\
                    .then_inc(wo_mm, 1)

            transposes(y, (2, 3), yT_mm, (norm_done, B))
            pe.wait_ge(wqkv2_in, 48)
            pe.wait_ge(yT_done, B)
            for k, w in enumerate((wq2, wk2, wv2)):
                for b in range(B):
                    product(ps[:, QKV_BANKS[B * k + b], :],
                            [(yT[:, kt, b * T:(b + 1) * T], w[:, kt, :]) for kt in range(KT)]).then_inc(qkv_mm, 1)
            pe.wait_ge(qkv_ready, 3 * B)
            for k, (src, sem_out) in enumerate(((Q2, q2T_mm), (K2, k2T_mm))):
                pe.wait_ge(scratch_in[k], 16)
                for g in range(G2):
                    last = pe.transpose(ps[:, 2 * k + g // 4, (g % 4) * P:(g % 4 + 1) * P],
                                        src[:, HPG * g:HPG * (g + 1), :].rearrange("p h d -> p (h d)"), ident[:])
                last.then_inc(sem_out, 1)
            pe.wait_ge(qt2_ready, 1)
            pe.wait_ge(km_ready, HPG)
            for g in range(G2 + 3):
                if g < G2:
                    if g >= 4:
                        pe.wait_ge(pt2_dve if g % 2 else pt2_act, (g - 4) // 2 + 1)
                    pe.matmul(ps[:, 4 + g % 4, :], QT2[:, g, :], KM[:, g, :, :].rearrange("p h t -> p (h t)"),
                              start=True, stop=True).then_inc(s2_mm, 1)
                if g >= 3:
                    pe.wait_ge(exp2_done, g - 3 + 1)
                    for i in range(HPG):
                        last = pe.transpose(ps[:, 4 + (g - 3) % 4, i * P:(i + 1) * P],
                                            P2[:, HPG * (g - 3) + i, :], ident[:])
                    last.then_inc(p2T_mm, 1)
            pe.wait_ge(pt2_act, G2 // 2)
            pe.wait_ge(pt2_dve, G2 // 2)
            pe.wait_ge(v2_ready, 2)
            for h in range(NH2):
                n = (h % 8) * (DH + 1)
                last = pe.matmul(ps[:, h // 8, n:n + DH + 1], PT2[:, h, :], V2[:, h, :], start=True, stop=True)
            last.then_inc(pv2_mm, 1)
            pe.wait_ge(c2_ready, 1)
            pe.wait_ge(scratch_in[3], 16)
            transposes(cn, (2, 3), cT_mm)
            pe.wait_ge(cT_done, B)
            pe.wait_ge(wo2_in, 16)
            for b in range(B):
                product(ps[:, 4 + b, :], [(cT[:, k, b * T:(b + 1) * T], wo2[:, k, :]) for k in range(KT)])\
                    .then_inc(o2_mm, 1)

            transposes(y, (2, 3), x2T_mm, (norm_done, 3 * B))
            pe.wait_ge(x2T_done, B)
            pe.wait_ge(wr_in, 16)
            for b in range(B):
                product(ps[:, 4 + b, 0:E], [(yT[:, k, b * T:(b + 1) * T], wr[:, k, :]) for k in range(KT)])\
                    .then_inc(logit_mm, 1)
            for e in range(E):
                for b in range(B):
                    pe.wait_ge(z_ready, B * e + b + 1)
                    if e:
                        pe.wait_ge(z_split, B * (e - 1) + b + 1)
                    for k in range(KT):
                        last = pe.transpose(ps[:, b, k * T:(k + 1) * T], zm[:, b, k * P:(k + 1) * P], ident[:])
                    last.then_inc(zT_mm, 1)
                if e == 0:
                    for b in range(B):
                        last = pe.transpose(ps[0:E, 6, b * T:(b + 1) * T], onehot[:, b, :], ident[:])
                    last.then_inc(ohT_mm, 1)

            pe.wait_ge(ohT_ready, 1)
            pe.wait_ge(b1_split, 2)
            pe.wait_ge(z_split, B * E)
            for b in range(B):
                for c in range(IC):
                    for n, part in enumerate((b1H, b1L)):
                        pe.matmul(ps[:, IC * b + c, :], ohT[:, b, :], part[:, c * CH:(c + 1) * CH],
                                  start=(n == 0), stop=False)
            for n in range(NW1):
                pe.wait_ge(w1_split, n + 1)
                wH, wL = w1H[n % 2], w1L[n % 2]
                for b in range(B):
                    t = slice(b * T, (b + 1) * T)
                    for c in range(IC):
                        cc = slice(c * CH, (c + 1) * CH)
                        dst = ps[:, IC * b + c, :]
                        pe.matmul(dst, zH[:, n, t], wH[:, cc], start=False, stop=False)
                        pe.matmul(dst, zH[:, n, t], wL[:, cc], start=False, stop=False)
                        last = pe.matmul(dst, zL[:, n, t], wH[:, cc], start=False, stop=(n == NW1 - 1))
                        if n == NW1 - 1:
                            last.then_inc(w1_mm, 1)
                if n < NW1 - 1:
                    last.then_inc(w1_tile, 1)

            for n in range(IT // 2):
                pe.wait_ge(gelu_done, IC + n // 2 + 1)
                if n >= 4:
                    pe.wait_ge(hT_dve if n % 2 else hT_act, (n - 4) // 2 + 1)
                for k in range(2):
                    for b in range(B):
                        last = pe.transpose(ps[:, n % 4, (B * k + b) * T:(B * k + b + 1) * T],
                                            hid[:, b, (2 * n + k) * P:(2 * n + k + 1) * P], ident[:])
                last.then_inc(hT_mm, 1)
            pe.wait_ge(gelu_done, B * IC)
            pe.wait_ge(hT_act, IT // 4)
            pe.wait_ge(hT_dve, IT // 4)
            pe.wait_ge(woF_in, 16)
            for b in range(B):
                product(ps[:, 4 + b, :], [(hidT[:, k, b * T:(b + 1) * T], woF[:, k, :]) for k in range(IT)])\
                    .then_inc(f_mm, 1)


ROWS = ("L0_xattn_bo", "L0_attn_bq", "L0_attn_bk", "L0_attn_bv", "L0_attn_bo", "L0_attn_gamma", "L0_attn_beta",
        "L0_ffn_bo", "L0_ffn_ln_gamma", "L0_ffn_ln_beta")


def kernel(**inputs):
    import numpy as np
    import concourse.bacc as bacc
    from concourse.bass_utils import run_bass_kernel_spmd

    v = {n: np.asarray(t) for n, t in inputs.items()}
    B, T, D = v["x"].shape
    CH = 512

    def tiles(w):
        return w.reshape(-1, P, w.shape[-1]).transpose(1, 0, 2)

    laid = {
        "x": v["x"],
        "ctxT": v["ctx_1024"].reshape(-1, CH, D // P, P).transpose(0, 3, 2, 1),
        "xWq": tiles(v["L0_xattn_Wq"]), "xWk": tiles(v["L0_xattn_Wk"]), "xWv": tiles(v["L0_xattn_Wv"]),
        "xWo": tiles(v["L0_xattn_Wo"]),
        "bias3": np.stack([v["L0_xattn_" + n].reshape(D // P, P).T for n in ("bq", "bk", "bv")], 1),
        "wq": tiles(v["L0_attn_wq"]), "wk": tiles(v["L0_attn_wk"]), "wv": tiles(v["L0_attn_wv"]),
        "wo": tiles(v["L0_attn_wo"]),
        "rows": np.stack([v[n] for n in ROWS]),
        "W_router": tiles(v["L0_ffn_W_router"]), "W1": v["L0_ffn_W1"], "b1": v["L0_ffn_b1"],
        "ffn_Wo": tiles(v["L0_ffn_Wo"]),
    }
    nc = bacc.Bacc("TRN2", target_bir_lowering=False, num_devices=1)
    arrays, aps = {}, {}
    for name, t in laid.items():
        t = np.ascontiguousarray(t)
        arrays["in_" + name] = t
        aps[name] = nc.dram_tensor("in_" + name, t.shape, mybir.dt.from_np(t.dtype), kind="ExternalInput").ap()
    out = nc.dram_tensor("out_dram", (B, T, D), F32, kind="ExternalOutput").ap()
    perceiver_block(nc, aps, out)
    r = run_bass_kernel_spmd(nc, [arrays], core_ids=[0])
    return r.results[0]["out_dram"]
```

```python
from contextlib import ExitStack

import concourse.bass as bass
from concourse import mybir

F32 = mybir.dt.float32
F32R = mybir.dt.float32r
ALU = mybir.AluOpType
ACT = mybir.ActivationFunctionType
AX = mybir.AxisListType

P = 128
KB = 1024
EPS = 1e-5
EPS_FFN = 1e-12


def perceiver_block(nc, a, out):
    B, T, D = a["x"].shape
    S = a["ctxT"].shape[0] // B * a["ctxT"].shape[3]
    H = 16
    DH = D // H
    KT = D // P
    HPG = P // DH
    G = H // HPG
    CH = a["ctxT"].shape[3]
    C = S // CH
    JT = CH // P
    NKT = S // P
    TOK = B * T
    E = a["W_router"].shape[2]
    I = a["W1"].shape[2]
    IT = I // P
    IC = I // CH
    NW1 = E * KT
    SCALE = float(DH) ** -0.5
    NH2 = B * H
    TPH = T // H
    G2 = NH2 // HPG
    assert G == JT and T == P and TPH * H == P and KT == G and IC * B == 8

    with ExitStack() as ctx:
        base = -(-nc.sbuf_base // 32) * 32
        ctx.enter_context(nc.sbuf_tensor("arena", [P, (207 * KB) // 4], F32))

        def at(name, shape, dtype, kb):
            return nc.alloc_sbuf_tensor_at(name, shape, dtype, offset=base + int(kb * KB))

        def sem(name):
            return ctx.enter_context(nc.semaphore(name))

        wkH = at("wkH", [P, KT, D], F32R, 0)
        wkL = at("wkL", [P, KT, D], F32R, 8)
        wvH = at("wvH", [P, KT, D], F32R, 16)
        wvL = at("wvL", [P, KT, D], F32R, 24)
        raw = at("raw", [P, KT, CH], F32, 32)
        ctxH = [at(f"ctxH{i}", [P, KT, CH], F32R, 40 + 8 * i) for i in range(2)]
        ctxL = [at(f"ctxL{i}", [P, KT, CH], F32R, 56 + 8 * i) for i in range(2)]
        PT = at("PT", [P, HPG, NKT, T], F32, 40)
        kH = at("kH", [P, G, S], F32R, 72)
        kL = at("kL", [P, G, S], F32R, 104)
        V = at("V", [P, NKT, D], F32, 136)
        Pm = [at(f"Pm{i}", [P, S], F32, kb) for i, kb in enumerate((168, 32))]
        qmH = at("qmH", [P, G, HPG, T], F32R, 176)
        qmL = at("qmL", [P, G, HPG, T], F32R, 184)
        x = at("x_sb", [P, B, D], F32, 192)
        qT = at("qT", [P, G, TOK], F32, 196)
        attnT = at("attnT", [P, G, TOK], F32, 200)
        ident = at("ident", [P, P], F32, 204)
        RT = at("RT", [P, T], F32, 204.5)
        rexp = at("rexp", [P, HPG, DH], F32, 205)
        small = at("small", [P, 384], F32, 205.5)
        wq = at("wq", [P, KT, D], F32, 136)
        wk_raw = at("wk_raw", [P, KT, D], F32, 144)
        wv_raw = at("wv_raw", [P, KT, D], F32, 152)
        xn = at("xn", [P, B, D], F32, 160)
        xnT = at("xnT", [P, KT, TOK], F32, 164)
        wo = at("wo", [P, KT, D], F32, 0)
        wq2 = at("wq2", [P, KT, D], F32, 8)
        wk2 = at("wk2", [P, KT, D], F32, 16)
        wv2 = at("wv2", [P, KT, D], F32, 24)
        wo2 = at("wo2", [P, KT, D], F32, 32)
        woF = at("woF", [P, IT, D], F32, 0)
        qkvn = at("qkvn", [P, B, 3, D], F32, 40)
        yT = at("yT", [P, KT, TOK], F32, 52)
        y = at("y", [P, B, D], F32, 56)
        cn = at("cn", [P, B, D], F32, 60)
        cT = at("cT", [P, KT, TOK], F32, 64)
        u = at("u", [P, B, D], F32, 68)
        yTH = at("yTH", [P, KT, TOK], F32R, 40)
        yTL = at("yTL", [P, KT, TOK], F32R, 44)
        resid = at("resid", [P, B, D], F32, 60)
        hidT = at("hidT", [P, IT, TOK], F32, 40)
        w1raw = [at(f"w1raw{i}", [P, I], F32, 72 + 8 * i) for i in range(2)]
        w1H = [at(f"w1H{i}", [P, I], F32R, 88 + 16 * i) for i in range(2)]
        w1L = [at(f"w1L{i}", [P, I], F32R, 96 + 16 * i) for i in range(2)]
        P2 = at("P2", [P, NH2, P], F32, 104)
        rows = at("rows", [P, 8, D], F32, 120)
        KM = at("KM", [P, G2, HPG, P], F32, 136)
        PT2 = at("PT2", [P, NH2, P], F32, 152)
        qkvp = at("qkvp", [P, B, 3, H, DH], F32, 168)
        c2 = [at(f"c2_{b}", [P, H, DH], F32, 168 + 6 * b) for b in range(B)]
        V2 = at("V2", [P, NH2, DH + 1], F32, 180)
        QT2 = at("QT2", [P, G2, P], F32, 185)
        zH = at("zH", [P, NW1, TOK], F32R, 136)
        zL = at("zL", [P, NW1, TOK], F32R, 152)
        b1raw = at("b1raw", [E, I], F32, 8)
        b1H = at("b1H", [E, I], F32R, 168)
        b1L = at("b1L", [E, I], F32R, 176)
        mask = at("mask", [P, E, TOK], F32, 185)
        ohT = at("ohT", [E, B, P], F32R, 189.5)
        wr = at("wr", [P, KT, E], F32, 191)
        hid = at("hid", [P, B, I], F32, 168)
        rowsA = at("rowsA", [P, 2, D], F32, 196)
        x2 = at("x2", [P, B, D], F32, 200)

        col = [0]

        def cols(n):
            col[0] += n
            assert col[0] <= 384
            return small[:, col[0] - n:col[0]]

        NLN = 5 * B
        stats = cols(NLN * 6).rearrange("p (n s) -> p n s", n=NLN)
        meanvar = cols(NLN * 2).rearrange("p (n s) -> p n s", n=NLN)
        vareps = cols(NLN)
        rstd = cols(NLN)
        minus_half = cols(1)
        bqs = cols(G)
        bias3 = cols(3 * G).rearrange("p (k g) -> p k g", k=3)
        mx = cols(2 * C).rearrange("p (k c) -> p k c", k=2)
        nmax = cols(2)
        den = cols(H * C).rearrange("p (h c) -> p h c", h=H)
        dsum = cols(HPG)
        recip = cols(HPG)
        mx2 = cols(NH2)
        recip2 = cols(NH2)
        logit = cols(B * E).rearrange("p (b e) -> p b e", b=B)
        lmax = cols(B)
        order = cols(E)
        rank = cols(B * E).rearrange("p (b e) -> p b e", b=B)
        rmax = cols(B)
        onehot = cols(B * E).rearrange("p (b e) -> p b e", b=B)

        ps = ctx.enter_context(nc.psum_tensor("ps", [P, 8, CH], F32))
        SB = 4
        PT_BANKS = (4, 5, 6)
        PT_ACT, PT_DVE = (0, 2), (1, 3)
        PV_BANK = 7
        QKV_BANKS = (4, 5, 6, 7, 0, 1)
        QK2_BANKS = (2, 0)
        CT_BANKS = (2, 0)

        x_in, wq_in, wk_in, wv_in, bias_in = (sem(n) for n in ("x_in", "wq_in", "wk_in", "wv_in", "bias_in"))
        raw_in = sem("raw_in")
        wo_in, wqkv2_in, wo2_in, rowsA_in, rows_in, w1_in0, w1_in1, woF_in, wr_in, b1_in = (
            sem(n) for n in ("wo_in", "wqkv2_in", "wo2_in", "rowsA_in", "rows_in", "w1_in0", "w1_in1", "woF_in", "wr_in", "b1_in"))
        w1_in = [w1_in0, w1_in1]
        ident_done, zero_done, half_done = sem("ident_done"), sem("zero_done"), sem("half_done")
        var_done, rstd_done, norm_done = sem("var_done"), sem("rstd_done"), sem("norm_done")
        xT_mm, xT_done, q_mm = sem("xT_mm"), sem("xT_done"), sem("q_mm")
        wk_split, wv_hi, wv_split, bq_scaled = sem("wk_split"), sem("wv_hi"), sem("wv_split"), sem("bq_scaled")
        ctx_hi, ctx_split = sem("ctx_hi"), sem("ctx_split")
        k_mm, k_hi, k_lo = sem("k_mm"), sem("k_hi"), sem("k_lo")
        v_mm = sem("v_mm")
        v_done = sem("v_done")
        qm_hi, qm_done = sem("qm_hi"), sem("qm_done")
        s_mm, max_part, max_done = sem("s_mm"), sem("max_part"), sem("max_done")
        exp_done, t_mm = sem("exp_done"), sem("t_mm")
        pt_act, pt_dve = sem("pt_act"), sem("pt_dve")
        pv_mm, rexp_done, r_mm, r_copied, o_done = (
            sem(n) for n in ("pv_mm", "rexp_done", "r_mm", "r_copied", "o_done"))
        dve_step = sem("dve_step")
        wo_mm, yT_mm, yT_done, qkv_mm, qkv_ready = (sem(n) for n in ("wo_mm", "yT_mm", "yT_done", "qkv_mm", "qkv_ready"))
        c2_ready, ones_ready, v2_ready, q2T_mm, k2T_mm = (sem(n) for n in ("c2_ready", "ones_ready", "v2_ready", "q2T_mm", "k2T_mm"))
        qt2_ready, km_zero, km_ready, s2_mm, sub2_done = (sem(n) for n in ("qt2_ready", "km_zero", "km_ready", "s2_mm", "sub2_done"))
        exp2_done, p2T_mm, pt2_act, pt2_dve, pv2_mm = (sem(n) for n in ("exp2_done", "p2T_mm", "pt2_act", "pt2_dve", "pv2_mm"))
        cT_mm, cT_done, o2_mm, x2T_mm, x2T_done = (sem(n) for n in ("cT_mm", "cT_done", "o2_mm", "x2T_mm", "x2T_done"))
        logit_mm, z_ready, ohT_mm, ohT_ready, zT_mm = (sem(n) for n in ("logit_mm", "z_ready", "ohT_mm", "ohT_ready", "zT_mm"))
        z_hi, z_split, w1_hi, w1_split, b1_hi = (sem(n) for n in ("z_hi", "z_split", "w1_hi", "w1_split", "b1_hi"))
        b1_split, w1_tile, w1_mm, gelu_done, hT_mm = (sem(n) for n in ("b1_split", "w1_tile", "w1_mm", "gelu_done", "hT_mm"))
        hT_act, hT_dve, f_mm, out_ready, stored = (sem(n) for n in ("hT_act", "hT_dve", "f_mm", "out_ready", "stored"))
        yT_hi, yT_lo, mask_mm, mask_done, resid_done = (
            sem(n) for n in ("yT_hi", "yT_lo", "mask_mm", "mask_done", "resid_done"))
        qkv_out, qkv_in = [sem(f"qkv_out{b}") for b in range(B)], [sem(f"qkv_in{b}") for b in range(B)]
        c2_out, c2_in = [sem(f"c2_out{b}") for b in range(B)], [sem(f"c2_in{b}") for b in range(B)]

        qkv_dram = nc.dram_tensor("qkv_dram", [B, 3, T, D], F32, kind="Internal").ap()
        c_dram = nc.dram_tensor("c_dram", [B, T, D], F32, kind="Internal").ap()
        qkv_by_token = [qkv_dram[b].rearrange("k t n -> t k n") for b in range(B)]
        qkv_by_position = [qkv_dram[b].rearrange("k (h t) (c d) -> (t c) k h d", t=TPH, d=DH) for b in range(B)]
        c_by_position = [c_dram[b].rearrange("(h t) (c d) -> (t c) h d", t=TPH, d=DH) for b in range(B)]

        block = ctx.enter_context(nc.Block())


        @block.sync
        def _(sp):
            sp.dma_start(x[:], a["x"].rearrange("b t d -> t b d")).then_inc(x_in, 16)
            sp.dma_start(bias3, a["bias3"]).then_inc(bias_in, 16)
            sp.dma_start(wk_raw[:], a["xWk"]).then_inc(wk_in, 16)
            sp.dma_start(wq[:], a["xWq"]).then_inc(wq_in, 16)
            sp.dma_start(raw[:], a["ctxT"][0]).then_inc(raw_in, 16)
            sp.dma_start(wv_raw[:], a["xWv"]).then_inc(wv_in, 16)
            for b in range(B):
                if b:
                    sp.wait_ge(t_mm, b * (H * C))
                    sp.dma_start(raw[:], a["ctxT"][b * C]).then_inc(raw_in, 16)
                with sp.Fori(b * C + 1, (b + 1) * C) as k:
                    sp.wait_ge(ctx_split, k)
                    sp.dma_start(raw[:], a["ctxT"][bass.ds(k, 1)].rearrange("a p k s -> (a p) k s")).then_inc(raw_in, 16)

            sp.wait_ge(v_mm, B * C * JT)
            sp.wait_ge(ctx_split, B * C)
            for t, n, s in ((wo, "xWo", wo_in), (wq2, "wq", wqkv2_in), (wk2, "wk", wqkv2_in),
                            (wv2, "wv", wqkv2_in)):
                sp.dma_start(t[:], a[n]).then_inc(s, 16)
            sp.wait_ge(qm_done, B * HPG)
            for n in range(2):
                sp.dma_start(rowsA[:, n, :], a["rows"][n:n + 1, :].to_broadcast([P, D])).then_inc(rowsA_in, 16)
            sp.wait_ge(s_mm, B * H * C)
            sp.dma_start(wr[:], a["W_router"]).then_inc(wr_in, 16)
            for n in range(8):
                sp.dma_start(rows[:, n, :], a["rows"][2 + n:3 + n, :].to_broadcast([P, D])).then_inc(rows_in, 16)
            w1_v = a["W1"].rearrange("e (k p) i -> (e k) p i", p=P)
            for n in range(2):
                sp.dma_start(w1raw[n][:], w1_v[n]).then_inc(w1_in[n], 16)
            sp.wait_ge(t_mm, B * H * C)
            sp.dma_start(wo2[:], a["wo"]).then_inc(wo2_in, 16)
            for b in range(B):
                sp.wait_ge(qkv_ready, 3 * (b + 1))
                sp.dma_start(qkv_by_token[b], qkvn[:, b, :, :]).then_inc(qkv_out[b], 16)
                sp.wait_ge(qkv_out[b], 16)
                sp.dma_start(qkvp[:, b, :, :, :], qkv_by_position[b]).then_inc(qkv_in[b], 16)
            sp.dma_start(b1raw[:], a["b1"]).then_inc(b1_in, 16)
            for b in range(B):
                sp.wait_ge(c2_ready, b + 1)
                sp.dma_start(c_by_position[b], c2[b][:]).then_inc(c2_out[b], 16)
                sp.wait_ge(c2_out[b], 16)
                sp.dma_start(cn[:, b, :], c_dram[b]).then_inc(c2_in[b], 16)
            for n in range(2, NW1):
                sp.wait_ge(w1_split, n - 1)
                sp.dma_start(w1raw[n % 2][:], w1_v[n]).then_inc(w1_in[n % 2], 16)
                if n == 3:
                    sp.wait_ge(o2_mm, B)
                    sp.wait_ge(b1_split, 2)
                    sp.dma_start(woF[:], a["ffn_Wo"]).then_inc(woF_in, 16)
            for b in range(B):
                sp.wait_ge(out_ready, b + 1)
                sp.dma_start(out[b], u[:, b, :]).then_inc(stored, 16)
            sp.wait_ge(stored, 16 * B)

        @block.gpsimd
        def _(pool):
            pool.memset(ident[:], 0.0).then_inc(ident_done, 1)
            pool.memset(minus_half, -0.5).then_inc(half_done, 1)
            pool.memset(qmH[:].bitcast(F32), 0.0).then_inc(zero_done, 1)
            pool.memset(qmL[:].bitcast(F32), 0.0).then_inc(zero_done, 1)
            for e in range(E):
                pool.memset(order[:, e:e + 1], float(E - e)).then_inc(half_done, 1)
            pool.wait_ge(ident_done, 1)
            pool.affine_select(out=ident[:], in_=ident[:], compare_op=ALU.not_equal, fill=1.0, base=0,
                               pattern=[[-1, P]], channel_multiplier=1).then_inc(ident_done, 1)

            def rsqrt(n):
                pool.wait_ge(half_done, 1 + E)
                pool.wait_ge(var_done, n + 1)
                pool.tensor_tensor(rstd[:, n:n + 1], vareps[:, n:n + 1], minus_half, ALU.pow).then_inc(rstd_done, 1)

            for b in range(B):
                rsqrt(b)
            pool.wait_ge(wv_hi, 1)
            pool.tensor_tensor(wvL[:], wv_raw[:], wvH[:].bitcast(F32), ALU.subtract).then_inc(wv_split, 1)
            pool.wait_ge(zero_done, 2)
            pool.wait_ge(wv_split, 1)
            pool.wait_ge(v_done, G)
            for b in range(B):
                if b:
                    pool.wait_ge(s_mm, b * (H * C))
                for i in range(HPG):
                    q = slice(DH * i, DH * (i + 1))
                    if b or i:
                        pool.wait_ge(qm_done, b * HPG + i)
                    pool.tensor_copy(qmH[q, :, i, :], qT[q, :, b * T:(b + 1) * T]).then_inc(qm_hi, 1)
                    pool.wait_ge(qm_hi, b * HPG + i + 1)
                    pool.tensor_tensor(qmL[q, :, i, :], qT[q, :, b * T:(b + 1) * T],
                                       qmH[q, :, i, :].bitcast(F32), ALU.subtract).then_inc(qm_done, 1)
            pool.wait_ge(qm_done, B * HPG)
            pool.wait_ge(pv_mm, B * G)
            pool.memset(KM[:], 0.0).then_inc(km_zero, 1)
            pool.wait_ge(km_zero, 1)
            for n in range(B, NLN):
                rsqrt(n)

        @block.scalar
        def _(act):
            for b in range(B):
                act.wait_ge(xT_mm, b + 1)
                act.copy(xnT[:, :, b * T:(b + 1) * T],
                         ps[:, b, :].rearrange("p (k t) -> p k t", k=KT)).then_inc(xT_done, 1)
            act.wait_ge(wv_in, 16)
            act.copy(wvH[:], wv_raw[:]).then_inc(wv_hi, 1)
            act.wait_ge(bq_scaled, 1)
            for m in range(G):
                act.wait_ge(q_mm, m + 1)
                act.activation(qT[:, m, :], ps[:, 4 + m, 0:TOK], ACT.Identity, bias=bqs[:, m:m + 1],
                               scale=SCALE).then_inc(v_done, 1)
            with act.Fori(0, B) as b:
                with act.Fori(0, C) as c:
                    for m in range(G):
                        act.wait_ge(k_mm, b * (C * G) + c * G + (m + 1))
                        act.activation(kH[:, m, bass.ds(c * CH, CH)], ps[:, m, :], ACT.Identity,
                                       bias=bias3[:, 1, m:m + 1]).then_inc(k_hi, 1)
                    for j in range(JT):
                        act.wait_ge(v_mm, b * (C * JT) + c * JT + (j + 1))
                        act.copy(V[:, bass.ds(c * JT + j, 1), :].rearrange("p a n -> p (a n)"), ps[:, 4 + j, :]).then_inc(v_done, 1)

                def pt_copy(h, c):
                    g, i = divmod(h, HPG)
                    act.wait_ge(t_mm, b * (H * C) + (C * h + c + 1))
                    if g == 0:
                        act.wait_ge(v_mm, (b + 1) * (C * JT))
                    else:
                        act.wait_ge(pv_mm, b * G + g)
                    act.copy(PT[:, i, c * JT:(c + 1) * JT, :].rearrange("p k t -> p (k t)"),
                             ps[:, PT_BANKS[(C * h + c) % len(PT_BANKS)], :]).then_inc(pt_act, 1)

                for h in range(H):
                    if h > 1 and h % HPG == 1:
                        act.wait_ge(r_mm, b * G + h // HPG)
                        act.copy(RT[:], ps[:, PV_BANK, P:2 * P]).then_inc(r_copied, 1)
                    for c in range(C):
                        if h and c in PT_ACT:
                            pt_copy(h - 1, c)
                        if h > 1:
                            act.wait_ge(t_mm, b * (H * C) + (C * (h - 2) + c + 1))
                        act.wait_ge(max_done, b * H + (h + 1))
                        act.activation(Pm[h % 2][:, c * CH:(c + 1) * CH], ps[:, (C * h + c) % SB, :], ACT.Exp,
                                       bias=nmax[:, h % 2:h % 2 + 1], accum_out=den[:, h, c:c + 1]).then_inc(exp_done, 1)
                for c in PT_ACT:
                    pt_copy(H - 1, c)
                act.wait_ge(r_mm, (b + 1) * G)
                act.copy(RT[:], ps[:, PV_BANK, P:2 * P]).then_inc(r_copied, 1)
                act.wait_ge(s_mm, (b + 1) * (H * C))
                act.wait_ge(pv_mm, (b + 1) * G)
                act.wait_ge(t_mm, (b + 1) * (H * C))

            def transposed(dst, sem_in, b, bank, sem_out):
                act.wait_ge(sem_in, b + 1)
                act.copy(dst[:, :, b * T:(b + 1) * T],
                         ps[:, bank, :].rearrange("p (k t) -> p k t", k=KT)).then_inc(sem_out, 1)

            for b in range(B):
                transposed(yT, yT_mm, b, 2 + b, yT_done)

            def queries2(b):
                act.wait_ge(q2T_mm, b + 1)
                act.copy(QT2[:, G * b:G * (b + 1), :].rearrange("p g t -> p (g t)"), ps[:, QK2_BANKS[b], :])\
                   .then_inc(qt2_ready, 1)

            queries2(0)
            for n in range(G2 + 3):
                if n == 2:
                    queries2(1)
                if n < G2:
                    act.wait_ge(sub2_done, n + 1)
                    act.activation(P2[:, HPG * n:HPG * (n + 1), :], P2[:, HPG * n:HPG * (n + 1), :],
                                   ACT.Exp, scale=SCALE).then_inc(exp2_done, 1)
                g = n - 3
                if g >= 0 and g % 2 == 0:
                    act.wait_ge(p2T_mm, g + 1)
                    act.copy(PT2[:, HPG * g:HPG * (g + 1), :].rearrange("p h t -> p (h t)"),
                             ps[:, 4 + g % 4, :]).then_inc(pt2_act, 1)
            for b in range(B):
                transposed(cT, cT_mm, b, CT_BANKS[b], cT_done)
            for b in range(B):
                transposed(yT, x2T_mm, b, 2 + b, x2T_done)
                transposed(yTH, x2T_mm, b, 2 + b, yT_hi)
            for n in range(E // 2):
                act.wait_ge(mask_mm, n + 1)
                act.copy(mask[:, 2 * n:2 * n + 2, :].rearrange("p e t -> p (e t)"), ps[:, 4 + n, :])\
                   .then_inc(mask_done, 1)
            for b in range(B):
                for c in range(IC):
                    act.wait_ge(w1_mm, IC * b + c + 1)
                    act.activation(hid[:, b, c * CH:(c + 1) * CH], ps[:, IC * b + c, :], ACT.Gelu)\
                       .then_inc(gelu_done, 1)
            for n in range(0, IT // 2, 2):
                act.wait_ge(hT_mm, n + 1)
                act.copy(hidT[:, 2 * n:2 * n + 2, :].rearrange("p k t -> p (k t)"), ps[:, n % 4, :])\
                   .then_inc(hT_act, 1)

        @block.vector
        def _(dve):
            steps = [0]

            def step(ins):
                steps[0] += 1
                ins.then_inc(dve_step, 1)
                dve.wait_ge(dve_step, steps[0])

            def statistics(src, eps, n):
                step(dve.bn_stats(stats[:, n, :], src))
                step(dve.bn_aggr(meanvar[:, n, :], stats[:, n, :]))
                dve.tensor_scalar(vareps[:, n:n + 1], meanvar[:, n, 1:2], eps, None, ALU.add).then_inc(var_done, 1)

            def normalize(src, dst, n):
                dve.wait_ge(rstd_done, n + 1)
                dve.tensor_scalar(dst, src, meanvar[:, n, 0:1], rstd[:, n:n + 1],
                                  ALU.subtract, ALU.mult).then_inc(norm_done, 1)

            dve.wait_ge(x_in, 16)
            for b in range(B):
                statistics(x[:, b, :], EPS, b)
            for b in range(B):
                normalize(x[:, b, :], xn[:, b, :], b)
            dve.wait_ge(wk_in, 16)
            step(dve.tensor_copy(wkH[:], wk_raw[:]))
            dve.tensor_tensor(wkL[:], wk_raw[:], wkH[:].bitcast(F32), ALU.subtract).then_inc(wk_split, 1)

            dve.wait_ge(bias_in, 16)
            dve.tensor_scalar(bqs, bias3[:, 0, :], SCALE, None, ALU.mult).then_inc(bq_scaled, 1)

            with dve.Fori(0, B) as b:
                def split(c):
                    dve.wait_ge(raw_in, b * (16 * C) + 16 * (c + 1))
                    if c >= 2:
                        dve.wait_ge(v_mm, b * (C * JT) + JT * (c - 1))
                    dve.tensor_copy(ctxH[c % 2][:], raw[:]).then_inc(ctx_hi, 1)
                    dve.wait_ge(ctx_hi, b * C + (c + 1))
                    dve.tensor_tensor(ctxL[c % 2][:], raw[:], ctxH[c % 2][:].bitcast(F32),
                                      ALU.subtract).then_inc(ctx_split, 1)

                split(0)
                for c in range(C):
                    if c + 1 < C:
                        split(c + 1)
                    for m in range(G):
                        dve.wait_ge(k_hi, b * (C * G) + (c * G + m + 1))
                        dve.scalar_tensor_tensor(out=kL[:, m, c * CH:(c + 1) * CH], in0=ps[:, m, :],
                                                 scalar=bias3[:, 1, m:m + 1],
                                                 in1=kH[:, m, c * CH:(c + 1) * CH].bitcast(F32),
                                                 op0=ALU.add, op1=ALU.subtract).then_inc(k_lo, 1)

                def maxima(h):
                    for c in range(C):
                        dve.wait_ge(s_mm, b * (H * C) + (C * h + c + 1))
                        dve.tensor_reduce(mx[:, h % 2, c:c + 1], ps[:, (C * h + c) % SB, :], AX.X, ALU.max).then_inc(max_part, 1)
                    dve.wait_ge(max_part, b * (H * C) + C * (h + 1))
                    dve.tensor_reduce(nmax[:, h % 2:h % 2 + 1], mx[:, h % 2, :], AX.X, ALU.max,
                                      negate=True).then_inc(max_done, 1)

                def pt_copies(h):
                    g, i = divmod(h, HPG)
                    for c in PT_DVE:
                        dve.wait_ge(t_mm, b * (H * C) + (C * h + c + 1))
                        if g == 0:
                            dve.wait_ge(v_mm, (b + 1) * (C * JT))
                        else:
                            dve.wait_ge(pv_mm, b * G + g)
                        dve.tensor_copy(PT[:, i, c * JT:(c + 1) * JT, :].rearrange("p k t -> p (k t)"),
                                        ps[:, PT_BANKS[(C * h + c) % len(PT_BANKS)], :]).then_inc(pt_dve, 1)

                def reciprocals(g):
                    dve.wait_ge(exp_done, b * (H * C) + C * HPG * (g + 1))
                    dve.tensor_reduce(dsum, den[:, HPG * g:HPG * (g + 1), :], AX.X, ALU.add).then_inc(rexp_done, 1)
                    dve.wait_ge(rexp_done, b * (3 * G) + (3 * g + 1))
                    dve.reciprocal(recip, dsum).then_inc(rexp_done, 1)
                    dve.wait_ge(rexp_done, b * (3 * G) + (3 * g + 2))
                    if g:
                        dve.wait_ge(r_mm, b * G + g)
                    dve.tensor_copy(rexp[:], recip.rearrange("p (h o) -> p h o", o=1).to_broadcast([P, HPG, DH]))\
                       .then_inc(rexp_done, 1)

                def outputs(g):
                    dve.wait_ge(r_copied, b * G + (g + 1))
                    dve.wait_ge(pv_mm, b * G + (g + 1))
                    dst = attnT[:, g, bass.ds(b * T, T)]
                    dve.tensor_tensor(dst, ps[:, PV_BANK, 0:T], RT[:], ALU.mult).then_inc(o_done, 1)
                    dve.wait_ge(o_done, b * (2 * G) + (2 * g + 1))
                    dve.tensor_scalar(dst, dst, bias3[:, 2, g:g + 1], None, ALU.add).then_inc(o_done, 1)

                for h in range(H):
                    maxima(h)
                    if h and h % HPG == 0:
                        reciprocals(h // HPG - 1)
                    if h:
                        pt_copies(h - 1)
                    if h > 1 and h % HPG == 1:
                        outputs(h // HPG - 1)
                reciprocals(G - 1)
                pt_copies(H - 1)
                outputs(G - 1)
                dve.wait_ge(pv_mm, (b + 1) * G)
                dve.wait_ge(r_mm, (b + 1) * G)

            names = ("bk", "bv", "bo", "beta", "gamma", "fbo", "fbeta", "fgamma")
            row = {n: rows[:, k, :] for k, n in enumerate(names)} | {"xbo": rowsA[:, 0, :], "bq": rowsA[:, 1, :]}
            dve.wait_ge(rowsA_in, 32)
            for b in range(B):
                step(dve.tensor_tensor(x[:, b, :], x[:, b, :], row["xbo"], ALU.add))
            for b in range(B):
                dve.wait_ge(wo_mm, b + 1)
                step(dve.tensor_tensor(x[:, b, :], ps[:, b, :], x[:, b, :], ALU.add))
                statistics(x[:, b, :], EPS, B + b)
                normalize(x[:, b, :], y[:, b, :], B + b)
            dve.wait_ge(rows_in, 8 * 16)
            for b in range(B):
                for k, bias in enumerate(("bq", "bk", "bv")):
                    dve.wait_ge(qkv_mm, 3 * b + k + 1)
                    dve.tensor_tensor(qkvn[:, b, k, :], ps[:, QKV_BANKS[3 * b + k], :], row[bias], ALU.add)\
                       .then_inc(qkv_ready, 1)
            dve.wait_ge(norm_done, 2 * B)
            for b in range(B):
                step(dve.tensor_tensor(u[:, b, :], y[:, b, :], row["bo"], ALU.add))
                step(dve.tensor_tensor(x[:, b, :], x[:, b, :], row["beta"], ALU.add))
            dve.memset(V2[:, :, DH:DH + 1], 1.0).then_inc(v2_ready, 1)

            def keys_and_values(b):
                dve.wait_ge(km_zero, 1)
                dve.wait_ge(k2T_mm, b + 1)
                kps = ps[:, QK2_BANKS[b] + 1, :].rearrange("p (g t) -> p g t", t=P)
                for i in range(HPG):
                    q = slice(DH * i, DH * (i + 1))
                    dve.tensor_copy(KM[q, G * b:G * (b + 1), i, :], kps[q, :, :]).then_inc(km_ready, 1)
                dve.wait_ge(qkv_in[b], 16)
                dve.tensor_copy(V2[:, H * b:H * (b + 1), 0:DH], qkvp[:, b, 2, :, :]).then_inc(v2_ready, 1)

            keys_and_values(0)
            for n in range(G2 + 3):
                if n == 2:
                    keys_and_values(1)
                if n < G2:
                    bank = ps[:, 4 + n % 4, :].rearrange("p (h t) -> p h t", h=HPG)
                    m = mx2[:, HPG * n:HPG * (n + 1)]
                    dve.wait_ge(s2_mm, n + 1)
                    step(dve.tensor_reduce(m, bank, AX.X, ALU.max))
                    dve.tensor_tensor(P2[:, HPG * n:HPG * (n + 1), :], bank,
                                      m.rearrange("p (h o) -> p h o", o=1).to_broadcast([P, HPG, P]),
                                      ALU.subtract).then_inc(sub2_done, 1)
                g = n - 3
                if g >= 0 and g % 2:
                    dve.wait_ge(p2T_mm, g + 1)
                    dve.tensor_copy(PT2[:, HPG * g:HPG * (g + 1), :].rearrange("p h t -> p (h t)"),
                                    ps[:, 4 + g % 4, :]).then_inc(pt2_dve, 1)
            for b in range(B):
                dve.wait_ge(pv2_mm, b + 1)
                o2 = ps[:, QK2_BANKS[b]:QK2_BANKS[b] + 2, 0:8 * (DH + 1)].rearrange("p a (h d) -> p a h d", h=8)
                r = recip2[:, H * b:H * (b + 1)].rearrange("p (a h o) -> p a h o", a=2, o=1)
                step(dve.reciprocal(r, o2[:, :, :, DH:DH + 1]))
                dve.tensor_tensor(c2[b][:].rearrange("p (a h) d -> p a h d", a=2), o2[:, :, :, 0:DH],
                                  r.to_broadcast([P, 2, 8, DH]), ALU.mult).then_inc(c2_ready, 1)

            def split_w1(n):
                dve.wait_ge(w1_in[n % 2], 16 * (n // 2 + 1))
                if n >= 2:
                    dve.wait_ge(w1_tile, n - 1)
                dve.tensor_copy(w1H[n % 2][:], w1raw[n % 2][:]).then_inc(w1_hi, 1)
                dve.wait_ge(w1_hi, n + 1)
                dve.tensor_tensor(w1L[n % 2][:], w1raw[n % 2][:], w1H[n % 2][:].bitcast(F32),
                                  ALU.subtract).then_inc(w1_split, 1)

            split_w1(0)
            for b in range(B):
                ub = u[:, b, :]
                dve.wait_ge(o2_mm, b + 1)
                step(dve.tensor_tensor(ub, ps[:, 4 + b, :], ub, ALU.add))
                statistics(ub, EPS, 2 * B + 2 * b)
                normalize(ub, ub, 2 * B + 2 * b)
                dve.wait_ge(norm_done, 2 * B + 2 * b + 1)
                step(dve.tensor_tensor(ub, ub, row["gamma"], ALU.mult))
                step(dve.tensor_tensor(x2[:, b, :], x[:, b, :], ub, ALU.add))
                statistics(x2[:, b, :], EPS, 2 * B + 2 * b + 1)
                normalize(x2[:, b, :], y[:, b, :], 2 * B + 2 * b + 1)
            dve.wait_ge(half_done, 1 + E)
            for b in range(B):
                dve.wait_ge(logit_mm, b + 1)
                step(dve.tensor_copy(logit[:, b, :], ps[:, 6 + b, 0:E]))
            wide = lambda t: t.rearrange("p (b o) -> p b o", o=1).to_broadcast([P, B, E])
            step(dve.tensor_reduce(lmax, logit, AX.X, ALU.max))
            step(dve.tensor_tensor(rank, logit, wide(lmax), ALU.is_ge))
            step(dve.tensor_tensor(rank, rank, order.rearrange("p (o e) -> p o e", o=1).to_broadcast([P, B, E]),
                                   ALU.mult))
            step(dve.tensor_reduce(rmax, rank, AX.X, ALU.max))
            dve.tensor_tensor(onehot, rank, wide(rmax), ALU.is_equal).then_inc(z_ready, 1)
            for b in range(B):
                t = slice(b * T, (b + 1) * T)
                dve.wait_ge(yT_hi, b + 1)
                dve.tensor_tensor(yTL[:, :, t], ps[:, 2 + b, :].rearrange("p (k t) -> p k t", k=KT),
                                  yTH[:, :, t].bitcast(F32), ALU.subtract).then_inc(yT_lo, 1)
            dve.wait_ge(b1_in, 16)
            dve.tensor_copy(b1H[:], b1raw[:]).then_inc(b1_split, 1)
            dve.wait_ge(b1_split, 1)
            dve.tensor_tensor(b1L[:], b1raw[:], b1H[:].bitcast(F32), ALU.subtract).then_inc(b1_split, 1)
            dve.wait_ge(ohT_mm, 1)
            dve.tensor_copy(ohT[:], ps[0:E, 1, 0:TOK].rearrange("p (b t) -> p b t", b=B)).then_inc(ohT_ready, 1)

            def masked_tokens(e):
                m = mask[:, e:e + 1, :].to_broadcast([P, KT, TOK])
                for z, t in ((zH, yTH), (zL, yTL)):
                    dve.tensor_tensor(z[:, KT * e:KT * (e + 1), :], t[:].bitcast(F32), m, ALU.mult)\
                       .then_inc(z_split, 1)

            dve.wait_ge(mask_done, E // 2)
            dve.wait_ge(yT_lo, B)
            masked_tokens(0)
            for n in range(1, NW1):
                split_w1(n)
                if n % KT == 1 and n // KT + 1 < E:
                    masked_tokens(n // KT + 1)
                if n == KT:
                    dve.wait_ge(norm_done, 4 * B)
                    for b in range(B):
                        step(dve.tensor_tensor(resid[:, b, :], y[:, b, :], row["fbo"], ALU.add))
                        step(dve.tensor_tensor(x2[:, b, :], x2[:, b, :], row["fbeta"], ALU.add))
            for n in range(1, IT // 2, 2):
                dve.wait_ge(hT_mm, n + 1)
                dve.tensor_copy(hidT[:, 2 * n:2 * n + 2, :].rearrange("p k t -> p (k t)"), ps[:, n % 4, :])\
                   .then_inc(hT_dve, 1)
            for b in range(B):
                ub = u[:, b, :]
                dve.wait_ge(f_mm, b + 1)
                step(dve.tensor_tensor(ub, ps[:, 4 + b, :], resid[:, b, :], ALU.add))
                statistics(ub, EPS_FFN, 4 * B + b)
                normalize(ub, ub, 4 * B + b)
                dve.wait_ge(norm_done, 4 * B + b + 1)
                step(dve.tensor_tensor(ub, ub, row["fgamma"], ALU.mult))
                dve.tensor_tensor(ub, x2[:, b, :], ub, ALU.add).then_inc(out_ready, 1)

        @block.tensor
        def _(pe):
            def transposes(src, b, bank, sem_out):
                for k in range(KT):
                    last = pe.transpose(ps[:, bank, k * T:(k + 1) * T], src[:, b, k * P:(k + 1) * P], ident[:])
                last.then_inc(sem_out, 1)

            def product(dst, pairs):
                for n, (l, r) in enumerate(pairs):
                    mm = pe.matmul(dst, l, r, start=(n == 0), stop=(n == len(pairs) - 1))
                return mm

            pe.wait_ge(ident_done, 2)
            for b in range(B):
                pe.wait_ge(norm_done, b + 1)
                transposes(xn, b, b, xT_mm)
            pe.wait_ge(xT_done, B)
            pe.wait_ge(wq_in, 16)
            for m in range(G):
                product(ps[:, 4 + m, 0:TOK], [(wq[:, k, m * P:(m + 1) * P], xnT[:, k, :]) for k in range(KT)])\
                    .then_inc(q_mm, 1)
            pe.wait_ge(wk_split, 1)
            pe.wait_ge(v_done, G)
            with pe.Fori(0, B) as b:
                with pe.Fori(0, C // 2) as cc:
                    for half in range(2):
                        cH, cL = ctxH[half], ctxL[half]
                        pe.wait_ge(ctx_split, b * C + cc * 2 + (half + 1))
                        for m in range(G):
                            f = slice(m * P, (m + 1) * P)
                            product(ps[:, m, :], [(w[:, k, f], c[:, k, :]) for k in range(KT)
                                                  for w, c in ((wkH, cH), (wkL, cH), (wkH, cL))]).then_inc(k_mm, 1)
                        pe.wait_ge(wv_split, 1)
                        pe.wait_ge(v_done, b * (C * JT) + cc * (2 * JT) + (half + 1) * JT)
                        for j in range(JT):
                            t = slice(j * P, (j + 1) * P)
                            product(ps[:, 4 + j, :], [(c[:, k, t], w[:, k, :]) for k in range(KT)
                                                      for c, w in ((cH, wvH), (cH, wvL), (cL, wvH))]).then_inc(v_mm, 1)
                        pe.wait_ge(k_lo, b * (C * G) + cc * (2 * G) + (half + 1) * G)

                pe.wait_ge(qm_done, (b + 1) * HPG)
                pe.wait_ge(v_done, (b + 1) * (C * JT) + JT)

                def scores(h):
                    g, i = divmod(h, HPG)
                    for c in range(C):
                        t = C * h + c
                        if t >= SB:
                            pe.wait_ge(exp_done, b * (H * C) + (t - SB + 1))
                        kk = slice(c * CH, (c + 1) * CH)
                        product(ps[:, t % SB, :], [(qmH[:, g, i, :], kH[:, g, kk]), (qmH[:, g, i, :], kL[:, g, kk]),
                                              (qmL[:, g, i, :], kH[:, g, kk])]).then_inc(s_mm, 1)

                def transpose_probs(h):
                    for c in range(C):
                        t = C * h + c
                        pe.wait_ge(exp_done, b * (H * C) + (t + 1))
                        if t >= len(PT_BANKS):
                            h0, c0 = divmod(t - len(PT_BANKS), C)
                            done, by = (pt_act, PT_ACT) if c0 in PT_ACT else (pt_dve, PT_DVE)
                            pe.wait_ge(done, b * (H * len(by)) + (h0 * len(by) + by.index(c0) + 1))
                        for j in range(JT):
                            last = pe.transpose(ps[:, PT_BANKS[t % len(PT_BANKS)], j * P:(j + 1) * P],
                                                Pm[h % 2][:, c * CH + j * P:c * CH + (j + 1) * P], ident[:])
                        last.then_inc(t_mm, 1)

                def weighted_values(g):
                    pe.wait_ge(pt_act, b * (H * len(PT_ACT)) + HPG * len(PT_ACT) * (g + 1))
                    pe.wait_ge(pt_dve, b * (H * len(PT_DVE)) + HPG * len(PT_DVE) * (g + 1))
                    if g:
                        pe.wait_ge(o_done, b * (2 * G) + 2 * g)
                    for n in range(NKT):
                        for i in range(HPG):
                            q = slice(DH * i, DH * (i + 1))
                            last = pe.matmul(ps[q, PV_BANK, 0:T], V[:, n, (HPG * g + i) * DH:(HPG * g + i + 1) * DH],
                                             PT[:, i, n, :], start=(n == 0), stop=(n == NKT - 1))
                    last.then_inc(pv_mm, 1)
                    pe.wait_ge(rexp_done, b * (3 * G) + 3 * (g + 1))
                    pe.matmul(ps[:, PV_BANK, P:2 * P], rexp[:].rearrange("p h d -> p (h d)"), ident[:],
                              start=True, stop=True).then_inc(r_mm, 1)

                for h in range(H):
                    scores(h)
                    if h > 1 and h % HPG == 1:
                        weighted_values(h // HPG - 1)
                    if h:
                        transpose_probs(h - 1)
                transpose_probs(H - 1)
                weighted_values(G - 1)
                pe.wait_ge(exp_done, (b + 1) * (H * C))
                pe.wait_ge(o_done, (b + 1) * (2 * G))

            pe.wait_ge(wo_in, 16)
            pe.wait_ge(o_done, B * 2 * G)
            pe.wait_ge(exp_done, B * H * C)
            for b in range(B):
                product(ps[:, b, :], [(attnT[:, k, b * T:(b + 1) * T], wo[:, k, :]) for k in range(KT)])\
                    .then_inc(wo_mm, 1)

            pe.wait_ge(wqkv2_in, 48)
            for b in range(B):
                pe.wait_ge(norm_done, B + b + 1)
                transposes(y, b, 2 + b, yT_mm)
            for b in range(B):
                pe.wait_ge(yT_done, b + 1)
                for k, w in enumerate((wq2, wk2, wv2)):
                    product(ps[:, QKV_BANKS[3 * b + k], :],
                            [(yT[:, kt, b * T:(b + 1) * T], w[:, kt, :]) for kt in range(KT)]).then_inc(qkv_mm, 1)

            def transpose_qk(b):
                pe.wait_ge(qkv_in[b], 16)
                for k, sem_out in enumerate((q2T_mm, k2T_mm)):
                    for g in range(G):
                        last = pe.transpose(ps[:, QK2_BANKS[b] + k, g * P:(g + 1) * P],
                                            qkvp[:, b, k, HPG * g:HPG * (g + 1), :].rearrange("p h d -> p (h d)"),
                                            ident[:])
                    last.then_inc(sem_out, 1)

            def outputs2(b):
                for h in range(H):
                    n = (h % 8) * (DH + 1)
                    last = pe.matmul(ps[:, QK2_BANKS[b] + h // 8, n:n + DH + 1], PT2[:, H * b + h, :],
                                     V2[:, H * b + h, :], start=True, stop=True)
                last.then_inc(pv2_mm, 1)

            pe.wait_ge(qkv_ready, 3 * B)
            transpose_qk(0)
            for g in range(G2 + 3):
                if g == 2:
                    transpose_qk(1)
                if g < G2:
                    if g % G == 0:
                        pe.wait_ge(qt2_ready, g // G + 1)
                        pe.wait_ge(km_ready, HPG * (g // G + 1))
                    if g >= 4:
                        pe.wait_ge(pt2_dve if g % 2 else pt2_act, (g - 4) // 2 + 1)
                    pe.matmul(ps[:, 4 + g % 4, :], QT2[:, g, :], KM[:, g, :, :].rearrange("p h t -> p (h t)"),
                              start=True, stop=True).then_inc(s2_mm, 1)
                if g >= 3:
                    pe.wait_ge(exp2_done, g - 3 + 1)
                    for i in range(HPG):
                        last = pe.transpose(ps[:, 4 + (g - 3) % 4, i * P:(i + 1) * P],
                                            P2[:, HPG * (g - 3) + i, :], ident[:])
                    last.then_inc(p2T_mm, 1)
                if g == G2:
                    pe.wait_ge(pt2_act, G // 2)
                    pe.wait_ge(pt2_dve, G // 2)
                    pe.wait_ge(v2_ready, 2)
                    outputs2(0)
            pe.wait_ge(pt2_act, G2 // 2)
            pe.wait_ge(pt2_dve, G2 // 2)
            pe.wait_ge(v2_ready, 3)
            outputs2(1)
            for b in range(B):
                pe.wait_ge(c2_ready, b + 1)
                pe.wait_ge(c2_in[b], 16)
                transposes(cn, b, CT_BANKS[b], cT_mm)
                pe.wait_ge(cT_done, b + 1)
                pe.wait_ge(wo2_in, 16)
                product(ps[:, 4 + b, :], [(cT[:, k, b * T:(b + 1) * T], wo2[:, k, :]) for k in range(KT)])\
                    .then_inc(o2_mm, 1)

            pe.wait_ge(wr_in, 16)
            for b in range(B):
                pe.wait_ge(norm_done, 2 * B + 2 * (b + 1))
                transposes(y, b, 2 + b, x2T_mm)
                pe.wait_ge(x2T_done, b + 1)
                product(ps[:, 6 + b, 0:E], [(yT[:, k, b * T:(b + 1) * T], wr[:, k, :]) for k in range(KT)])\
                    .then_inc(logit_mm, 1)
            pe.wait_ge(z_ready, 1)
            for e in range(E):
                for b in range(B):
                    last = pe.matmul(ps[:, 4 + e // 2, (e % 2) * TOK + b * T:(e % 2) * TOK + (b + 1) * T],
                                     onehot[:, b, e:e + 1].to_broadcast([P, P]), ident[:], start=True, stop=True)
                if e % 2:
                    last.then_inc(mask_mm, 1)
            for b in range(B):
                last = pe.transpose(ps[0:E, 1, b * T:(b + 1) * T], onehot[:, b, :], ident[:])
            last.then_inc(ohT_mm, 1)

            pe.wait_ge(ohT_ready, 1)
            pe.wait_ge(b1_split, 2)
            pe.wait_ge(mask_done, E // 2)
            pe.wait_ge(yT_lo, B)
            for b in range(B):
                for c in range(IC):
                    for n, part in enumerate((b1H, b1L)):
                        pe.matmul(ps[:, IC * b + c, :], ohT[:, b, :], part[:, c * CH:(c + 1) * CH],
                                  start=(n == 0), stop=False)
            for n in range(NW1):
                pe.wait_ge(z_split, 2 * (n // KT + 1))
                pe.wait_ge(w1_split, n + 1)
                wH, wL = w1H[n % 2], w1L[n % 2]
                for b in range(B):
                    t = slice(b * T, (b + 1) * T)
                    for c in range(IC):
                        cc = slice(c * CH, (c + 1) * CH)
                        dst = ps[:, IC * b + c, :]
                        pe.matmul(dst, zH[:, n, t], wH[:, cc], start=False, stop=False)
                        pe.matmul(dst, zH[:, n, t], wL[:, cc], start=False, stop=False)
                        last = pe.matmul(dst, zL[:, n, t], wH[:, cc], start=False, stop=(n == NW1 - 1))
                        if n == NW1 - 1:
                            last.then_inc(w1_mm, 1)
                if n < NW1 - 1:
                    last.then_inc(w1_tile, 1)

            for n in range(IT // 2):
                pe.wait_ge(gelu_done, IC + n // 2 + 1)
                if n >= 4:
                    pe.wait_ge(hT_dve if n % 2 else hT_act, (n - 4) // 2 + 1)
                for k in range(2):
                    for b in range(B):
                        last = pe.transpose(ps[:, n % 4, (B * k + b) * T:(B * k + b + 1) * T],
                                            hid[:, b, (2 * n + k) * P:(2 * n + k + 1) * P], ident[:])
                last.then_inc(hT_mm, 1)
            pe.wait_ge(gelu_done, B * IC)
            pe.wait_ge(hT_act, IT // 4)
            pe.wait_ge(hT_dve, IT // 4)
            pe.wait_ge(woF_in, 16)
            for b in range(B):
                product(ps[:, 4 + b, :], [(hidT[:, k, b * T:(b + 1) * T], woF[:, k, :]) for k in range(IT)])\
                    .then_inc(f_mm, 1)


ROWS = ("L0_xattn_bo", "L0_attn_bq", "L0_attn_bk", "L0_attn_bv", "L0_attn_bo", "L0_attn_beta", "L0_attn_gamma",
        "L0_ffn_bo", "L0_ffn_ln_beta", "L0_ffn_ln_gamma")


def kernel(**inputs):
    import numpy as np
    import concourse.bacc as bacc
    from concourse.bass_utils import run_bass_kernel_spmd

    v = {n: np.asarray(t) for n, t in inputs.items()}
    B, T, D = v["x"].shape
    CH = 512

    def tiles(w):
        return w.reshape(-1, P, w.shape[-1]).transpose(1, 0, 2)

    laid = {
        "x": v["x"],
        "ctxT": v["ctx_1024"].reshape(-1, CH, D // P, P).transpose(0, 3, 2, 1),
        "xWq": tiles(v["L0_xattn_Wq"]), "xWk": tiles(v["L0_xattn_Wk"]), "xWv": tiles(v["L0_xattn_Wv"]),
        "xWo": tiles(v["L0_xattn_Wo"]),
        "bias3": np.stack([v["L0_xattn_" + n].reshape(D // P, P).T for n in ("bq", "bk", "bv")], 1),
        "wq": tiles(v["L0_attn_wq"]), "wk": tiles(v["L0_attn_wk"]), "wv": tiles(v["L0_attn_wv"]),
        "wo": tiles(v["L0_attn_wo"]),
        "rows": np.stack([v[n] for n in ROWS]),
        "W_router": tiles(v["L0_ffn_W_router"]), "W1": v["L0_ffn_W1"], "b1": v["L0_ffn_b1"],
        "ffn_Wo": tiles(v["L0_ffn_Wo"]),
    }
    nc = bacc.Bacc("TRN2", target_bir_lowering=False, num_devices=1)
    arrays, aps = {}, {}
    for name, t in laid.items():
        t = np.ascontiguousarray(t)
        arrays["in_" + name] = t
        aps[name] = nc.dram_tensor("in_" + name, t.shape, mybir.dt.from_np(t.dtype), kind="ExternalInput").ap()
    out = nc.dram_tensor("out_dram", (B, T, D), F32, kind="ExternalOutput").ap()
    perceiver_block(nc, aps, out)
    r = run_bass_kernel_spmd(nc, [arrays], core_ids=[0])
    return r.results[0]["out_dram"]
```
